# Optimizing a Trainium2 kernel written in Bass

```python
import numpy as np
import jax
import jax.numpy as jnp

def _softmax(x, axis=-1):
    return jax.nn.softmax(x, axis=axis)

def _gelu(x):
    return jax.nn.gelu(x, approximate=True)

def _silu(x):
    return jax.nn.silu(x)

def _sigmoid(x):
    return jax.nn.sigmoid(x)

def _layernorm(x, axis=-1, eps=1e-05):
    m = jnp.mean(x, axis=axis, keepdims=True)
    v = jnp.var(x, axis=axis, keepdims=True)
    return (x - m) / jnp.sqrt(v + eps)

def _scatter_add(tgt, idx, src, axis=0):
    return tgt.at[idx].add(src)

def _segment_sum(src, seg, n):
    return jax.ops.segment_sum(src, seg, n)
kernel_name = 'mk_adj_preln_d2_adj_r2_426c06'

def setup_inputs(seed: int=0):
    np.random.seed(seed)
    _w = jnp.asarray

    def _rec_inputs():
        import jax
        import jax.numpy as jnp
        _gk = jax.random.key(seed)
        x = -0.000929 + 1 * jax.random.normal(jax.random.fold_in(_gk, 1), (8192, 64), jnp.float32)
        _a = jax.random.bernoulli(jax.random.fold_in(_gk, 2), 0.000244141, (8192, 8192))
        _a = jnp.logical_or(_a, jnp.eye(8192, dtype=bool))
        _af = _a.astype(jnp.float32)
        _af = _af * jax.random.uniform(jax.random.fold_in(_gk, 3), (8192, 8192), jnp.float32, 0.05, 1)
        adj = _af
        return (x, adj)
    x, adj = _rec_inputs()

    def _L0_gnn_setup():
        import jax, jax.numpy as jnp
        import numpy as np
        HOP = 2
        N = 8192
        HIDDEN = 64
        key = jax.random.key(seed)
        k1, k2, k3 = jax.random.split(key, 3)
        user_embs = jax.random.normal(k1, (N, HIDDEN), dtype=jnp.float32)
        adj = jax.random.uniform(k2, (N, N), dtype=jnp.float32)
        limit = float(np.sqrt(6.0 / (2 * HIDDEN + HIDDEN)))
        W = jax.random.uniform(k3, (HOP, 2 * HIDDEN, HIDDEN), dtype=jnp.float32, minval=-limit, maxval=limit)
        return {'user_embs': user_embs, 'adj': adj, 'W': W}
    _L0_gnn_all = _L0_gnn_setup()
    _L0_gnn_in = {k: v for k, v in _L0_gnn_all.items() if k in ('W',)}
    del _L0_gnn_all

    def _L1_gnn_setup():
        import jax, jax.numpy as jnp
        import numpy as np
        N = 8192
        NFEAT = 64
        NHID = 64
        key = jax.random.key(seed)
        k1, k2, k3, k4 = jax.random.split(key, 4)
        x = jax.random.normal(k1, (N, NFEAT), dtype=jnp.float32)
        adj_matrix = jax.random.uniform(k2, (N, N), dtype=jnp.float32)
        degree_norm = jax.random.uniform(k3, (N, 1), dtype=jnp.float32)
        W = jax.random.normal(k4, (NFEAT, NHID), dtype=jnp.float32) / np.sqrt(NFEAT)
        b = jnp.zeros((NHID,), dtype=jnp.float32)
        return {'x': x, 'adj_matrix': adj_matrix, 'degree_norm': degree_norm, 'W': W, 'b': b}
    _L1_gnn_all = _L1_gnn_setup()
    _L1_gnn_in = {k: v for k, v in _L1_gnn_all.items() if k in ('W', 'b')}
    del _L1_gnn_all
    return {'x': x, 'adj': adj, 'L0_gnn_W': _L0_gnn_in['W'], 'L1_gnn_W': _L1_gnn_in['W'], 'L1_gnn_b': _L1_gnn_in['b']}

def reference(x, adj, L0_gnn_W, L1_gnn_W, L1_gnn_b):
    import jax
    import jax.numpy as jnp

    def _L0_gnn_ref(user_embs, adj, W):
        import jax, jax.numpy as jnp
        import numpy as np
        HOP = 2
        N = 8192
        HIDDEN = 64
        x = user_embs
        for k in range(HOP):
            agg = adj @ x
            x = jnp.tanh(jnp.concatenate([agg, x], axis=1) @ W[k])
        return x

    def _L1_gnn_ref(x, adj_matrix, degree_norm, W, b):
        import jax, jax.numpy as jnp
        import numpy as np
        N = 8192
        NFEAT = 64
        NHID = 64
        neighbor_sum = adj_matrix @ x
        sub = x - degree_norm * neighbor_sum
        h = sub @ W + b
        return jax.nn.relu(h)
    deg = jnp.maximum((adj != 0).astype(jnp.float32).sum(-1), 1.0)
    deg = deg ** (-0.5)
    h = jnp.maximum(_layernorm(x, axis=-1), 0.0)
    x = x + _L0_gnn_ref(h, adj, L0_gnn_W)
    h = jnp.maximum(_layernorm(x, axis=-1), 0.0)
    x = x + _L1_gnn_ref(h, adj, deg[..., None], L1_gnn_W, L1_gnn_b)
    return x

_drawn_inputs = setup_inputs


def setup_inputs(seed=0):
    import zlib

    import numpy as np

    out = dict(_drawn_inputs(seed))
    spreads = {'L1_gnn_b': (0.0, 0.1)}
    factors = {}
    for name, (base, spread) in spreads.items():
        noise = np.random.default_rng([zlib.crc32(name.encode()), seed]).standard_normal(out[name].shape)
        drawn = base * np.exp(spread * noise) if base else spread * noise
        out[name] = jnp.asarray(drawn.astype(out[name].dtype))
    for name, factor in factors.items():
        out[name] = (out[name] * factor).astype(out[name].dtype)
    return out
```

```python
import concourse.bass as bass
from concourse import mybir
from contextlib import ExitStack

F32 = mybir.dt.float32
BF16 = mybir.dt.bfloat16
ALU = mybir.AluOpType
ACT = mybir.ActivationFunctionType
AX = mybir.AxisListType

P = 128
F = 64
BLK = 1024
KT = BLK // P
HALF = 512
EPS = 1e-5


def gnn_program(nc, x_d, adj_d, w0_d, w1_d, w3_d, b_d, out_d):
    NB = x_d.shape[1] // (KT * F)
    GW = KT * F
    COUNTS = 4 * NB + 1
    PASS2 = NB * NB
    PASS3 = PASS2 + NB * (NB - 1) // 2

    def block_at(row, j):
        return NB * row + j

    def block_at2(q, j, skipped=0):
        return PASS2 - skipped + ((q * (q - 1)) >> 1) + j

    def block_at3(t, j, skipped=0):
        before = (t * (2 * NB + 1 - t)) >> 1
        if not isinstance(t, int):
            before = before & (NB * NB - 1)
        return PASS3 - skipped + before + j

    def wrap(i):
        return i & (NB - 1)

    def settled(eng, value):
        return value if isinstance(value, int) else eng.snap(eng.to_reg(value))

    ctx = ExitStack()
    with ctx:
        def sb(name, shape, dt=F32):
            return ctx.enter_context(nc.sbuf_tensor(name, shape, dt))

        def pb(name, shape):
            return ctx.enter_context(nc.psum_tensor(name, shape, F32))

        def sem(name):
            return ctx.enter_context(nc.semaphore(name))

        ring = sb("ring", [P, KT, BLK])
        diag = sb("diag", [P, KT, BLK])
        cat = sb("cat", [P, NB * KT * 2 * F])
        feat = sb("feat", [P, NB * BLK])
        xres = sb("xres", [P, NB * GW])
        stage = [sb(f"stage{h}", [P, 4 * 2 * F]) for h in range(2)]
        act_out = sb("act_out", [P, GW])
        norm_out = sb("norm_out", [P, GW])
        cat_t = sb("cat_t", [P, BLK])
        agg_t = sb("agg_t", [P, BLK])
        centred = sb("centred", [P, GW])
        square = sb("square", [P, GW])
        total = sb("total", [P, KT])
        negmean = sb("negmean", [P, KT])
        sqsum = sb("sqsum", [P, KT])
        var = sb("var", [P, KT])
        rstd = sb("rstd", [P, KT])
        tally = sb("tally", [P, 2 * BLK], BF16)
        tally_out = sb("tally_out", [P, 2 * BLK], BF16)
        degree = sb("degree", [P, NB * KT])
        degree1 = sb("degree1", [P, NB * KT])
        invroot = sb("invroot", [P, NB * KT])
        neg_invroot = sb("neg_invroot", [P, NB * KT])
        minus_half = sb("minus_half", [P, NB * KT])
        w0x = sb("w0x", [P, F])
        w0a = sb("w0a", [F, F])
        w1x = sb("w1x", [P, F])
        w3 = sb("w3", [P, F])
        bias = sb("bias", [P, F])
        ident = sb("ident", [P, P])
        zeros = sb("zeros", [P, HALF], BF16)
        ones = sb("ones", [P, 1], BF16)

        main = pb("main", [P, BLK])
        odd = pb("odd", [P, BLK])
        own = pb("own", [P, BLK])
        dense = pb("dense", [P, HALF])
        turned = pb("turned", [P, HALF])

        ring_full = [sem(f"ring_full{s}") for s in range(KT)]
        diag_full = [sem(f"diag_full{c}") for c in range(KT // 2)]
        x_in = [sem(f"x_in{g}") for g in range(NB)]
        weights_in = sem("weights_in")
        out_stored = sem("out_stored")
        const_made = sem("const_made")
        cat_cleared = sem("cat_cleared")
        ktile_read = sem("ktile_read")
        dense_done = sem("dense_done")
        turned_done = sem("turned_done")
        own_done = sem("own_done")
        counts_done = sem("counts_done")
        staged = sem("staged")
        act_ready = sem("act_ready")
        x1_kept = sem("x1_kept")
        turned_kept = sem("turned_kept")
        drained1 = sem("drained1")
        cat_t_in = sem("cat_t_in")
        drained2 = sem("drained2")
        part_kept = sem("part_kept")
        h2_kept = sem("h2_kept")
        drained3 = sem("drained3")
        h_ready = sem("h_ready")
        norm_step = sem("norm_step")
        counted = sem("counted")
        count_read = sem("count_read")
        own_added = sem("own_added")
        part_cleared = sem("part_cleared")
        agg2_in = sem("agg2_in")
        y_ready = sem("y_ready")
        h2_ready = sem("h2_ready")
        degree_ready = sem("degree_ready")
        agg3_in = sem("agg3_in")
        out_step = sem("out_step")
        rstd_ready = sem("rstd_ready")
        invroot_ready = sem("invroot_ready")

        block = ctx.enter_context(nc.Block())

        def rows_of(buf, lo, hi, r):
            return buf[lo:hi, bass.ds(r * BLK, BLK)]

        def nodes_of(buf, r):
            return buf[:, bass.ds(r * GW, GW)].rearrange("p (k c) -> p k c", c=F)

        def cat_of(r, half):
            v = cat[:, bass.ds(r * KT * 2 * F, KT * 2 * F)].rearrange("p (k c) -> p k c", c=2 * F)
            return v[:, :, half * F:(half + 1) * F]

        def by_tile(buf):
            return buf[:, :].rearrange("p (k c) -> p k c", c=F)

        def spread(small):
            return small.unsqueeze(2).to_broadcast([P, KT, F])

        @block.sync
        def _(sp):
            def load(tile, s):
                sp.dma_start(ring[:, s, :], adj_d[tile]).then_inc(ring_full[s], 16)

            def load_block(row, col, block, steps=None):
                tile0, read0 = settled(sp, (row * NB + col) * KT), settled(sp, KT * block)
                for s in range(KT):
                    tile, read = settled(sp, tile0 + s), settled(sp, read0 + s + 1)
                    if steps is not None:
                        seen = settled(sp, steps + s // 2 + 1)
                        sp.wait_ge(counted, seen)
                    sp.wait_ge(ktile_read, read)
                    load(tile, s)

            def load_diag(row):
                first = row * (NB + 1) * KT
                if not isinstance(row, int):
                    first, free, seen = settled(sp, first), settled(sp, row), settled(sp, COUNTS * row)
                    sp.wait_ge(own_done, free)
                    sp.wait_ge(counted, seen)
                for c in range(KT // 2):
                    src = adj_d[bass.ds(first + 2 * c, 2)]
                    sp.dma_start(diag[:, 2 * c:2 * c + 2, :], src.rearrange("s p r -> p s r")).then_inc(diag_full[c], 16)

            def load_x(g):
                sp.dma_start(xres[:, g * GW:(g + 1) * GW], x_d[:, g * GW:(g + 1) * GW]).then_inc(x_in[g], 16)

            load_x(1)
            load_x(2 % NB)
            for s in range(KT):
                load(KT + s, s)
                if s < NB - 2:
                    load_x((s + 3) % NB)
            for dst, src in ((w0x[0:F, :], w0_d[F:2 * F, :]), (w0x[F:P, :], w0_d[0:F, :]), (w0a[:, :], w0_d[0:F, :]),
                             (w1x[0:F, :], w1_d[F:2 * F, :]), (w1x[F:P, :], w1_d[0:F, :]),
                             (w3[0:F, :], w3_d[:, :]), (w3[F:P, :], w3_d[:, :]),
                             (bias[:, :], b_d.partition_broadcast(P))):
                sp.dma_start(dst, src).then_inc(weights_in, 16)

            def ring_row(row):
                with sp.Fori(1, NB - 1) as j:
                    load_block(row, wrap(row + 1 + j), block_at(row, j) - 1, COUNTS * row + 1 + 4 * (j - 1))

            ring_row(0)
            load_diag(0)
            with sp.Fori(1, NB) as row:
                load_block(row, wrap(row + 1), block_at(row, 0) - 2, COUNTS * row - 8)
                ring_row(row)
                load_diag(row)

            load_block(NB - 2, NB - 1, PASS2 - 2, COUNTS * NB - 8)
            with sp.Fori(2, NB) as q:
                with sp.Fori(0, q) as j:
                    load_block(NB - 1 - q, NB - 1 - j, block_at2(q, j) - 1)
            with sp.Fori(0, NB) as t:
                with sp.Fori(0, NB - t) as j:
                    load_block(NB - 1 - t, wrap(NB - 1 - t - j), block_at3(t, j) - 1)

        @block.tensor
        def _(pe):
            def open_banks(bufs):
                for buf in bufs:
                    for hf in range(2):
                        nc.tensor.matmul(buf[:, hf * HALF:(hf + 1) * HALF], zeros[:, 0:P], zeros[:, :],
                                         start=True, stop=False, skip_group_check=True)

            def stream_block(g, tile_of, full, both):
                for pair in range(KT // 2):
                    st = stage[pair // 2]
                    if pair % 2 == 0:
                        pe.wait_ge(staged, 2 * g + pair // 2 + 1)
                    for s in (2 * pair, 2 * pair + 1):
                        full(s)
                        if both:
                            for hf in range(2):
                                mm = nc.tensor.matmul(main[:, hf * HALF:(hf + 1) * HALF],
                                                      st[:, (s % 4) * P:(s % 4 + 1) * P],
                                                      tile_of(s)[:, hf * HALF:(hf + 1) * HALF],
                                                      start=False, stop=False, skip_group_check=True)
                            mm.then_inc(ktile_read, 1)
                    if not both:
                        for hf in range(2):
                            for s in (2 * pair, 2 * pair + 1):
                                half = s % 2
                                mm = nc.tensor.matmul((main, odd)[half][half * F:(half + 1) * F, hf * HALF:(hf + 1) * HALF],
                                                      st[:, (s % 4) * P:(s % 4) * P + F],
                                                      tile_of(s)[:, hf * HALF:(hf + 1) * HALF],
                                                      start=False, stop=False, skip_group_check=True)
                                if hf == 1:
                                    mm.then_inc(ktile_read, 1)

            def stream_ring(g, n, both):
                stream_block(g, lambda s: ring[:, s, :],
                             lambda s: pe.wait_ge(ring_full[s], 16 * n + 16), both)

            def transposes(tiles):
                for k in range(KT):
                    lo = (k % 2) * F
                    mm = nc.tensor.matmul(turned[lo:lo + F, (k // 2) * P:(k // 2 + 1) * P], tiles(k), ident[:, :],
                                          start=True, stop=True, skip_group_check=True)
                mm.then_inc(turned_done, 1)

            def dense_product(terms, dst):
                for k in range(KT):
                    for i, (lhs, rhs) in enumerate(terms):
                        mm = nc.tensor.matmul(dst[:, k * F:(k + 1) * F], lhs[:, k * P:(k + 1) * P], rhs,
                                              start=(i == 0), stop=(i == len(terms) - 1), skip_group_check=True)
                return mm

            def own_tile(k):
                return act_out[:, k * F:(k + 1) * F]

            def x1_product(row):
                pe.wait_ge(turned_kept, 4 * row + 2)
                pe.wait_ge(count_read, row + 1)
                dense_product([(cat_t[:, :], w0x[:, :]), (agg_t[0:F, :], w0a[:, :])], dense).then_inc(dense_done, 1)

            def own_block(row):
                pe.wait_ge(act_ready, row + 1)
                pe.wait_ge(turned_kept, 4 * row + 2)
                transposes(own_tile)
                pe.wait_ge(own_added, 2 * row + 2)
                for pair in range(KT // 2):
                    for hf in range(2):
                        for half in range(2):
                            k = 2 * pair + half
                            mm = nc.tensor.matmul(own[half * F:(half + 1) * F, hf * HALF:(hf + 1) * HALF], own_tile(k),
                                                  diag[:, k, hf * HALF:(hf + 1) * HALF],
                                                  start=(pair == 0), stop=(pair == KT // 2 - 1), skip_group_check=True)
                mm.then_inc(own_done, 1)
                pe.wait_ge(counted, COUNTS * row + COUNTS)
                for k in range(KT):
                    for half in range(2):
                        lo = half * BLK + k * P
                        mm = nc.tensor.matmul(dense[:, k:k + 1], tally_out[:, lo:lo + P], ones[:, :],
                                              start=(half == 0), stop=(half == 1), skip_group_check=True)
                mm.then_inc(counts_done, 1)

            def diagonal(row):
                stream_block(block_at(row, NB - 1), lambda s: diag[:, s, :],
                             lambda s: pe.wait_ge(diag_full[s // 2], 16 * row + 16), False)
                pe.wait_ge(turned_kept, 4 * row)
                transposes(lambda k: stage[k // 4][:, (k % 4) * P:(k % 4) * P + F])

            def right_blocks(row):
                with pe.Fori(0, NB - 1 - row) as j:
                    stream_ring(block_at(row, j), (NB - 1) * row + j, False)

            pe.wait_ge(const_made, 4)
            open_banks((main, odd))
            right_blocks(0)
            diagonal(0)
            pe.wait_ge(weights_in, 8 * 16)
            with pe.Fori(1, NB) as row:
                pe.wait_ge(drained1, 3 * row)
                open_banks((main, odd))
                x1_product(row - 1)
                with pe.If(row < NB - 1):
                    right_blocks(row)
                own_block(row - 1)
                with pe.Fori(0, row) as col:
                    stream_ring((NB - 1) * row + NB - 1 + col, (NB - 2) * row + NB - 1 + col, True)
                diagonal(row)
            pe.wait_ge(drained1, 3 * NB)
            open_banks((main,))
            x1_product(NB - 1)
            own_block(NB - 1)

            def x2_product(q):
                pe.wait_ge(cat_t_in, q)
                pe.wait_ge(agg2_in, q)
                dense_product([(cat_t[:, :], w1x[:, :])], dense).then_inc(dense_done, 1)

            def h2_transposes(q):
                pe.wait_ge(h2_ready, q)
                pe.wait_ge(turned_kept, 4 * NB + 2 * (q - 1))
                transposes(lambda k: norm_out[:, k * F:(k + 1) * F])

            pe.wait_ge(count_read, NB + 1)
            x2_product(1)
            h2_transposes(1)
            stream_ring(PASS2, PASS2 - NB, True)
            with pe.Fori(2, NB) as q:
                pe.wait_ge(drained2, q - 1)
                pe.wait_ge(agg2_in, q)
                open_banks((main,))
                x2_product(q)
                with pe.Fori(0, q - 1) as j:
                    stream_ring(block_at2(q, j), block_at2(q, j, NB), True)
                h2_transposes(q)
                stream_ring(block_at2(q, q - 1), block_at2(q, q - 1, NB), True)

            def out_product(t):
                pe.wait_ge(cat_t_in, NB + 1 + t)
                pe.wait_ge(drained3, t + 1)
                pe.wait_ge(agg3_in, t + 1)
                pe.wait_ge(out_step, 4 * t + 4)
                dense_product([(cat_t[0:F, :], w3[0:F, :])], dense)
                dense_product([(agg_t[:, :], w3[:, :])], turned).then_inc(dense_done, 1)

            pe.wait_ge(drained2, NB - 1)
            pe.wait_ge(agg2_in, NB)
            open_banks((main, odd))
            x2_product(NB)
            with pe.Fori(0, NB) as j:
                stream_ring(block_at3(0, j), block_at3(0, j, NB), False)
            h2_transposes(NB)
            pe.wait_ge(turned_kept, 6 * NB)
            with pe.Fori(1, NB) as t:
                pe.wait_ge(drained3, t)
                pe.wait_ge(agg3_in, t)
                open_banks((main, odd))
                out_product(t - 1)
                with pe.Fori(0, NB - t) as j:
                    stream_ring(block_at3(t, j), block_at3(t, j, NB), False)
            out_product(NB - 1)

        @block.scalar
        def _(act):
            def stage_block(g, col, free=True, width=2 * F):
                src = cat[:, bass.ds(col * KT * 2 * F, KT * 2 * F)].rearrange("p (k c) -> p k c", c=2 * F)
                for h in range(2):
                    if free:
                        act.wait_ge(ktile_read, KT * (g - 1) + 4 * (h + 1))
                    dst = stage[h][:, :].rearrange("p (k c) -> p k c", c=2 * F)
                    nc.scalar.copy(dst[:, :, 0:width], src[:, 4 * h:4 * h + 4, 0:width]).then_inc(staged, 1)

            def tanh_rows(done):
                act.wait_ge(dense_done, done)
                nc.scalar.activation(act_out[:, :], dense[:, :], ACT.Tanh).then_inc(act_ready, 1)

            def keep_x1(row):
                act.wait_ge(act_ready, row + 1)
                nc.scalar.copy(cat_of(row, 1), by_tile(act_out)).then_inc(x1_kept, 1)

            def keep_turned(count, dst):
                act.wait_ge(turned_done, count)
                tiles = dst.rearrange("p (m two c) -> p two m c", two=2, c=P)
                for half in range(2):
                    src = turned[half * F:(half + 1) * F, :].rearrange("p (m c) -> p m c", c=P)
                    nc.scalar.copy(tiles[:, half], src).then_inc(turned_kept, 1)

            def drain_row(row):
                act.wait_ge(ktile_read, KT * NB * row + KT * NB)
                nc.scalar.copy(agg_t[0:F, :], main[0:F, :]).then_inc(drained1, 1)
                nc.scalar.copy(cat_t[F:P, :], odd[F:P, :]).then_inc(drained1, 1)
                nc.scalar.copy(rows_of(feat, F, P, row), main[F:P, :]).then_inc(drained1, 1)

            act.wait_ge(cat_cleared, 1)
            act.wait_ge(h_ready, 1)
            stage_block(0, 1, free=False)
            with act.Fori(1, NB - 1) as j:
                act.wait_ge(h_ready, j + 1)
                stage_block(block_at(0, j), j + 1)
            act.wait_ge(h_ready, NB)
            stage_block(block_at(0, NB - 1), 0)
            keep_turned(1, cat_t[0:F, :])
            drain_row(0)
            with act.Fori(1, NB) as row:
                act.wait_ge(turned_done, 2 * row - 1)
                stage_block(block_at(row, 0), wrap(row + 1))
                tanh_rows(row)
                keep_x1(row - 1)
                act.wait_ge(x1_kept, row)
                with act.Fori(1, NB - 1) as j:
                    stage_block(block_at(row, j), wrap(row + 1 + j))
                stage_block(block_at(row, NB - 1), row)
                keep_turned(2 * row, rows_of(feat, 0, F, row - 1))
                keep_turned(2 * row + 1, cat_t[0:F, :])
                drain_row(row)
            tanh_rows(NB)
            keep_x1(NB - 1)
            keep_turned(2 * NB, rows_of(feat, 0, F, NB - 1))

            def bring_features(value, row):
                act.wait_ge(dense_done, value)
                nc.scalar.copy(cat_t[0:F, :], rows_of(feat, 0, F, row)).then_inc(cat_t_in, 1)

            def keep_part(q):
                act.wait_ge(drained2, q - 1)
                act.wait_ge(agg2_in, q)
                nc.scalar.copy(rows_of(feat, F, P, NB - q), agg_t[F:P, :]).then_inc(part_kept, 1)

            def keep_h2(q):
                act.wait_ge(h2_ready, q)
                nc.scalar.copy(cat_of(NB - q, 0), by_tile(norm_out)).then_inc(h2_kept, 1)
                act.wait_ge(h2_kept, q)

            act.wait_ge(turned_kept, 4 * NB)
            act.wait_ge(x1_kept, NB)
            bring_features(NB, NB - 1)
            act.wait_ge(own_done, NB)
            tanh_rows(NB + 1)
            keep_h2(1)
            act.wait_ge(turned_done, 2 * NB - 1)
            stage_block(PASS2, NB - 1)
            keep_turned(2 * NB + 1, rows_of(feat, 0, F, NB - 1))
            bring_features(NB + 1, NB - 2)

            def drain_partial(q):
                act.wait_ge(ktile_read, KT * block_at2(q + 1, 0))
                nc.scalar.copy(agg_t[F:P, :], main[0:F, :]).then_inc(drained2, 1)

            drain_partial(1)
            with act.Fori(2, NB) as q:
                stage_block(block_at2(q, 0), NB - 1)
                act.wait_ge(y_ready, q - 1)
                tanh_rows(NB + q)
                keep_part(q)
                with act.If(q > 2):
                    with act.Fori(1, q - 1) as j:
                        stage_block(block_at2(q, j), NB - 1 - j)
                keep_h2(q)
                stage_block(block_at2(q, q - 1), wrap(NB - q))
                keep_turned(2 * NB + q, rows_of(feat, 0, F, NB - q))
                bring_features(NB + q, NB - 1 - q)
                act.wait_ge(part_kept, q - 1)
                drain_partial(q)

            def drain_even(t):
                act.wait_ge(ktile_read, KT * block_at3(t + 1, 0))
                nc.scalar.copy(agg_t[0:F, :], main[0:F, :]).then_inc(drained3, 1)

            stage_block(block_at3(0, 0), NB - 1, width=F)
            act.wait_ge(y_ready, NB - 1)
            tanh_rows(2 * NB)
            keep_part(NB)
            with act.Fori(1, NB - 1) as j:
                stage_block(block_at3(0, j), NB - 1 - j, width=F)
            keep_h2(NB)
            stage_block(block_at3(0, NB - 1), 0, width=F)
            keep_turned(3 * NB, rows_of(feat, 0, F, 0))
            bring_features(2 * NB, NB - 1)
            drain_even(0)
            act.wait_ge(turned_kept, 6 * NB)
            with act.Fori(1, NB) as t:
                with act.Fori(0, NB - t) as j:
                    stage_block(block_at3(t, j), wrap(NB - 1 - t - j), width=F)
                bring_features(2 * NB + t, NB - 1 - t)
                drain_even(t)

        @block.vector
        def _(dve):
            def norm_first(i, src):
                def after(k):
                    dve.wait_ge(norm_step, 6 * i + k)

                nc.vector.tensor_reduce(total[:, :], src, AX.X, ALU.add).then_inc(norm_step, 1)
                after(1)
                nc.vector.tensor_scalar(negmean[:, :], total[:, :], -1.0 / F, None, ALU.mult).then_inc(norm_step, 1)
                after(2)
                nc.vector.tensor_tensor(by_tile(centred), src, spread(negmean[:, :]), ALU.add).then_inc(norm_step, 1)
                after(3)
                nc.vector.tensor_tensor(by_tile(square), by_tile(centred), by_tile(centred), ALU.mult).then_inc(norm_step, 1)
                after(4)
                nc.vector.tensor_reduce(sqsum[:, :], by_tile(square), AX.X, ALU.add).then_inc(norm_step, 1)
                after(5)
                nc.vector.tensor_scalar(var[:, :], sqsum[:, :], 1.0 / F, EPS, ALU.mult, ALU.add).then_inc(norm_step, 1)

            def norm_last(i, dst):
                dve.wait_ge(rstd_ready, i + 1)
                return nc.vector.scalar_tensor_tensor(out=dst, in0=by_tile(centred), scalar=0.0,
                                                      in1=spread(rstd[:, :]), op0=ALU.max, op1=ALU.mult)

            def count(done, dst, tiles):
                dve.wait_ge(counted, done)
                nc.vector.scalar_tensor_tensor(out=dst[:, :], in0=tiles.rearrange("p s r -> p (s r)"), scalar=0.0,
                                               in1=tally[:, :], op0=ALU.not_equal, op1=ALU.add).then_inc(counted, 1)

            def count_ring(row, j):
                for c in range(KT // 2):
                    for s in (2 * c, 2 * c + 1):
                        dve.wait_ge(ring_full[s], 16 * ((NB - 1) * row + j) + 16)
                    count(COUNTS * row + 1 + 4 * j + c, tally, ring[:, 2 * c:2 * c + 2, :])

            def count_diag(row):
                for c in range(KT // 2):
                    dve.wait_ge(diag_full[c], 16 * row + 16)
                    dst = tally if c < KT // 2 - 1 else tally_out
                    count(COUNTS * row + 1 + 4 * (NB - 1) + c, dst, diag[:, 2 * c:2 * c + 2, :])

            def take_counts(row):
                dve.wait_ge(counts_done, row + 1)
                nc.vector.tensor_copy(degree[:, bass.ds(row * KT, KT)], dense[:, 0:KT]).then_inc(count_read, 1)

            def add_own(row):
                dve.wait_ge(own_done, row + 1)
                dve.wait_ge(drained1, 3 * row + 3)
                part = rows_of(feat, F, P, row)
                nc.vector.tensor_tensor(part, part, own[F:P, :], ALU.add).then_inc(own_added, 1)
                dve.wait_ge(own_added, 2 * row + 3)
                nc.vector.tensor_tensor(part, part, own[0:F, :], ALU.add).then_inc(own_added, 1)

            dve.sem_inc(count_read, 1)
            dve.sem_inc(own_added, 2)
            dve.sem_inc(out_step, 4)

            def x_first(i, g):
                dve.wait_ge(x_in[g], 16)
                norm_first(i, nodes_of(xres, g))

            nc.vector.memset(cat[:, :].rearrange("p (k c) -> p k c", c=2 * F)[:, :, F:2 * F], 0.0).then_inc(cat_cleared, 1)
            x_first(0, 1)
            nc.vector.memset(tally[:, :], 0.0).then_inc(counted, 1)
            norm_last(0, cat_of(1, 0)).then_inc(h_ready, 1)
            for j in range(NB - 1):
                x_first(j + 1, (j + 2) % NB)
                count_ring(0, j)
                norm_last(j + 1, cat_of((j + 2) % NB, 0)).then_inc(h_ready, 1)
            count_diag(0)
            with dve.Fori(1, NB) as row:
                dve.wait_ge(counted, COUNTS * row)
                nc.vector.memset(tally[:, :], 0.0).then_inc(counted, 1)
                with dve.Fori(0, NB - 1) as j:
                    count_ring(row, j)
                dve.wait_ge(counts_done, row)
                count_diag(row)
                take_counts(row - 1)
                add_own(row - 1)
            take_counts(NB - 1)
            add_own(NB - 1)

            def y_and_norm(q, row):
                y = nodes_of(xres, row)
                dve.wait_ge(act_ready, NB + q)
                nc.vector.tensor_tensor(y, y, by_tile(act_out), ALU.add).then_inc(y_ready, 1)
                dve.wait_ge(y_ready, q)
                norm_first(NB + q - 1, nodes_of(xres, wrap(row)))

            def h2_rows(q):
                norm_last(NB + q - 1, by_tile(norm_out)).then_inc(h2_ready, 1)

            dve.wait_ge(own_added, 2 * NB + 2)
            dve.wait_ge(dense_done, NB)
            nc.vector.tensor_copy(cat_t[F:P, :], rows_of(feat, F, P, NB - 1)).then_inc(agg2_in, 1)
            dve.wait_ge(agg2_in, 1)
            nc.vector.memset(rows_of(feat, F, P, NB - 1), 0.0).then_inc(part_cleared, 1)
            y_and_norm(1, NB - 1)
            h2_rows(1)
            dve.wait_ge(count_read, NB + 1)
            nc.vector.tensor_scalar(degree1[:, :], degree[:, :], 1.0, None, ALU.max).then_inc(degree_ready, 1)
            with dve.Fori(2, NB + 1) as q:
                row = settled(dve, NB - q)
                dve.wait_ge(ktile_read, KT * block_at2(q, 0))
                dve.wait_ge(dense_done, NB + q - 1)
                nc.vector.tensor_tensor(cat_t[F:P, :], rows_of(feat, F, P, row), main[F:P, :],
                                        ALU.add).then_inc(agg2_in, 1)
                y_and_norm(q, row)
                dve.wait_ge(h2_kept, q - 1)
                dve.wait_ge(turned_done, 2 * NB + q - 1)
                h2_rows(q)
            dve.wait_ge(invroot_ready, 1)
            nc.vector.tensor_scalar(neg_invroot[:, :], invroot[:, :], -1.0, None, ALU.mult).then_inc(degree_ready, 1)
            dve.wait_ge(part_cleared, 1)
            dve.wait_ge(degree_ready, 2)

            with dve.Fori(0, NB) as t:
                row = settled(dve, NB - 1 - t)
                dve.wait_ge(ktile_read, KT * block_at3(t + 1, 0))
                dve.wait_ge(part_kept, NB - 1)
                dve.wait_ge(dense_done, 2 * NB + t)
                nc.vector.tensor_tensor(agg_t[F:P, :], rows_of(feat, F, P, row), odd[F:P, :],
                                        ALU.add).then_inc(agg3_in, 1)
                dve.wait_ge(dense_done, 2 * NB + 1 + t)
                scale = neg_invroot[:, bass.ds(row * KT, KT)].unsqueeze(2).to_broadcast([P, KT, F])
                nc.vector.tensor_tensor(by_tile(square), by_tile(turned), scale, ALU.mult).then_inc(out_step, 1)
                dve.wait_ge(out_step, 4 * t + 5)
                nc.vector.tensor_tensor(centred[:, :], square[:, :], dense[:, :], ALU.add).then_inc(out_step, 1)
                dve.wait_ge(out_step, 4 * t + 6)
                nc.vector.tensor_tensor(by_tile(square), by_tile(centred),
                                        bias[:, :].unsqueeze(1).to_broadcast([P, KT, F]), ALU.add).then_inc(out_step, 1)
                dve.wait_ge(out_step, 4 * t + 7)
                y = nodes_of(xres, row)
                nc.vector.scalar_tensor_tensor(out=y, in0=by_tile(square), scalar=0.0, in1=y,
                                               op0=ALU.max, op1=ALU.add).then_inc(out_step, 1)

        @block.gpsimd
        def _(pool):
            nc.gpsimd.memset(ident[:, :], 0.0).then_inc(const_made, 1)
            nc.gpsimd.memset(zeros[:, :], 0.0).then_inc(const_made, 1)
            nc.gpsimd.memset(ones[:, :], 1.0).then_inc(const_made, 1)
            pool.wait_ge(const_made, 3)
            nc.gpsimd.affine_select(out=ident[:, :], in_=ident[:, :], compare_op=ALU.not_equal, fill=1.0, base=0,
                                    pattern=[[-1, P]], channel_multiplier=1).then_inc(const_made, 1)
            nc.gpsimd.memset(minus_half[:, :], -0.5).then_inc(const_made, 1)
            pool.wait_ge(const_made, 5)

            def power(i):
                pool.wait_ge(norm_step, 6 * i + 6)
                nc.gpsimd.tensor_tensor(rstd[:, :], var[:, :], minus_half[:, 0:KT], ALU.pow).then_inc(rstd_ready, 1)

            with pool.Fori(0, NB + 1) as i:
                power(i)
            pool.wait_ge(degree_ready, 1)
            nc.gpsimd.tensor_tensor(invroot[:, :], degree1[:, :], minus_half[:, :], ALU.pow).then_inc(invroot_ready, 1)
            with pool.Fori(NB + 1, 2 * NB) as i:
                power(i)
            with pool.Fori(0, NB) as t:
                first = settled(pool, (NB - 1 - t) * GW)
                pool.wait_ge(out_step, 4 * t + 8)
                rows = bass.ds(first, GW)
                pool.dma_start(out_d[:, rows], xres[:, rows]).then_inc(out_stored, 16)
            pool.wait_ge(out_stored, 16 * NB)


def kernel(**inputs):
    import numpy as np
    import concourse.bacc as bacc
    from concourse.bass_utils import run_bass_kernel_spmd

    n, f = inputs["x"].shape
    nb = n // BLK

    def node_major(a):
        return np.ascontiguousarray(a.reshape(n // P, P, f).transpose(1, 0, 2).reshape(P, -1))

    adj = np.asarray(inputs["adj"]).reshape(nb, BLK, nb, KT, P)
    arrays = {
        "x": node_major(np.asarray(inputs["x"])),
        "adj": np.ascontiguousarray(adj.transpose(0, 2, 3, 4, 1)).reshape(nb * nb * KT, P, BLK),
        "w0": np.ascontiguousarray(inputs["L0_gnn_W"][0]),
        "w1": np.ascontiguousarray(inputs["L0_gnn_W"][1]),
        "w3": np.ascontiguousarray(inputs["L1_gnn_W"]),
        "b": np.ascontiguousarray(inputs["L1_gnn_b"]),
    }
    nc = bacc.Bacc("TRN2", target_bir_lowering=False, num_devices=1)
    args = [nc.dram_tensor("in_" + name, a.shape, mybir.dt.from_np(a.dtype), kind="ExternalInput").ap()
            for name, a in arrays.items()]
    out = nc.dram_tensor("out", (P, n // P * f), F32, kind="ExternalOutput").ap()
    gnn_program(nc, *args, out)
    r = run_bass_kernel_spmd(nc, [{"in_" + name: a for name, a in arrays.items()}], core_ids=[0])
    return r.results[0]["out"].reshape(P, n // P, f).transpose(1, 0, 2).reshape(n, f)
```

```python
import concourse.bass as bass
from concourse import mybir
from contextlib import ExitStack, nullcontext

F32 = mybir.dt.float32
BF16 = mybir.dt.bfloat16
ALU = mybir.AluOpType
ACT = mybir.ActivationFunctionType
AX = mybir.AxisListType

P = 128
F = 64
BLK = 1024
KT = BLK // P
HALF = 512
EPS = 1e-5


def gnn_program(nc, x_d, adj_d, w0_d, w1_d, w3_d, b_d, out_d):
    NB = x_d.shape[1] // (KT * F)
    GW = KT * F
    COUNTS = 4 * NB + 1
    PASS2 = NB * NB
    PASS3 = PASS2 + NB * (NB - 1) // 2

    def block_at(row, j):
        return NB * row + j

    def block_at2(q, j, skipped=0):
        return PASS2 - skipped + ((q * (q - 1)) >> 1) + j

    def block_at3(t, j, skipped=0):
        before = (t * (2 * NB + 1 - t)) >> 1
        if not isinstance(t, int):
            before = before & (NB * NB - 1)
        return PASS3 - skipped + before + j

    def wrap(i):
        return i & (NB - 1)

    def settled(eng, value):
        return value if isinstance(value, int) else eng.snap(eng.to_reg(value))

    ctx = ExitStack()
    with ctx:
        def sb(name, shape, dt=F32):
            return ctx.enter_context(nc.sbuf_tensor(name, shape, dt))

        def pb(name, shape):
            return ctx.enter_context(nc.psum_tensor(name, shape, F32))

        def sem(name):
            return ctx.enter_context(nc.semaphore(name))

        ring = sb("ring", [P, KT, BLK])
        diag = sb("diag", [P, KT, BLK])
        cat = sb("cat", [P, NB * KT * 2 * F])
        feat = sb("feat", [P, NB * BLK])
        xres = sb("xres", [P, NB * GW])
        stage = [sb(f"stage{h}", [P, 4 * 2 * F]) for h in range(2)]
        act_out = sb("act_out", [P, GW])
        norm_out = sb("norm_out", [P, GW])
        cat_t = sb("cat_t", [P, BLK])
        agg_t = sb("agg_t", [P, BLK])
        centred = sb("centred", [P, GW])
        square = sb("square", [P, GW])
        total = sb("total", [P, KT])
        negmean = sb("negmean", [P, KT])
        sqsum = sb("sqsum", [P, KT])
        var = sb("var", [P, KT])
        rstd = sb("rstd", [P, KT])
        tally = sb("tally", [P, 2 * BLK], BF16)
        tally_out = sb("tally_out", [P, 2 * BLK], BF16)
        degree = sb("degree", [P, NB * KT])
        degree1 = sb("degree1", [P, NB * KT])
        invroot = sb("invroot", [P, NB * KT])
        neg_invroot = sb("neg_invroot", [P, NB * KT])
        minus_half = sb("minus_half", [P, NB * KT])
        w0x = sb("w0x", [P, F])
        w0a = sb("w0a", [F, F])
        w1x = sb("w1x", [P, F])
        w3 = sb("w3", [P, F])
        bias = sb("bias", [P, F])
        ident = sb("ident", [P, P])
        zeros = sb("zeros", [P, HALF], BF16)
        ones = sb("ones", [P, 1], BF16)

        main = pb("main", [P, BLK])
        odd = pb("odd", [P, BLK])
        own = pb("own", [P, BLK])
        dense = pb("dense", [P, HALF])
        turned = pb("turned", [P, HALF])

        ring_full = [sem(f"ring_full{s}") for s in range(KT)]
        diag_full = [sem(f"diag_full{c}") for c in range(KT // 2)]
        x_in = [sem(f"x_in{g}") for g in range(NB)]
        weights_in = sem("weights_in")
        out_stored = sem("out_stored")
        const_made = sem("const_made")
        cat_cleared = sem("cat_cleared")
        ktile_read = sem("ktile_read")
        dense_done = sem("dense_done")
        turned_done = sem("turned_done")
        own_done = sem("own_done")
        counts_done = sem("counts_done")
        staged = sem("staged")
        act_ready = sem("act_ready")
        x1_kept = sem("x1_kept")
        turned_kept = sem("turned_kept")
        drained1 = sem("drained1")
        cat_t_in = sem("cat_t_in")
        drained2 = sem("drained2")
        part_kept = sem("part_kept")
        h2_kept = sem("h2_kept")
        drained3 = sem("drained3")
        h_ready = sem("h_ready")
        norm_step = sem("norm_step")
        counted = sem("counted")
        count_read = sem("count_read")
        odd_drained = sem("odd_drained")
        own_added = sem("own_added")
        part_cleared = sem("part_cleared")
        agg2_in = sem("agg2_in")
        y_ready = sem("y_ready")
        h2_ready = sem("h2_ready")
        degree_ready = sem("degree_ready")
        agg3_in = sem("agg3_in")
        out_step = sem("out_step")
        rstd_ready = sem("rstd_ready")
        invroot_ready = sem("invroot_ready")

        block = ctx.enter_context(nc.Block())

        def rows_of(buf, lo, hi, r):
            return buf[lo:hi, bass.ds(r * BLK, BLK)]

        def nodes_of(buf, r):
            return buf[:, bass.ds(r * GW, GW)].rearrange("p (k c) -> p k c", c=F)

        def cat_of(r, half):
            v = cat[:, bass.ds(r * KT * 2 * F, KT * 2 * F)].rearrange("p (k c) -> p k c", c=2 * F)
            return v[:, :, half * F:(half + 1) * F]

        def by_tile(buf):
            return buf[:, :].rearrange("p (k c) -> p k c", c=F)

        def spread(small):
            return small.unsqueeze(2).to_broadcast([P, KT, F])

        @block.sync
        def _(sp):
            def load(tile, s):
                sp.dma_start(ring[:, s, :], adj_d[tile]).then_inc(ring_full[s], 16)

            def load_block(row, col, block, steps=None):
                tile0, read0 = settled(sp, (row * NB + col) * KT), settled(sp, KT * block)
                for s in range(KT):
                    tile, read = settled(sp, tile0 + s), settled(sp, read0 + s + 1)
                    if steps is not None:
                        seen = settled(sp, steps + s // 2 + 1)
                        sp.wait_ge(counted, seen)
                    sp.wait_ge(ktile_read, read)
                    load(tile, s)

            def load_diag(row):
                first = row * (NB + 1) * KT
                if not isinstance(row, int):
                    first, free, seen = settled(sp, first), settled(sp, row), settled(sp, COUNTS * row)
                    sp.wait_ge(own_done, free)
                    sp.wait_ge(counted, seen)
                for c in range(KT // 2):
                    src = adj_d[bass.ds(first + 2 * c, 2)]
                    sp.dma_start(diag[:, 2 * c:2 * c + 2, :], src.rearrange("s p r -> p s r")).then_inc(diag_full[c], 16)

            def load_x(g):
                sp.dma_start(xres[:, g * GW:(g + 1) * GW], x_d[:, g * GW:(g + 1) * GW]).then_inc(x_in[g], 16)

            load_x(1)
            load_x(2 % NB)
            for s in range(KT):
                load(KT + s, s)
                if s < NB - 2:
                    load_x((s + 3) % NB)
            for dst, src in ((w0x[0:F, :], w0_d[F:2 * F, :]), (w0x[F:P, :], w0_d[0:F, :]), (w0a[:, :], w0_d[0:F, :]),
                             (w1x[0:F, :], w1_d[F:2 * F, :]), (w1x[F:P, :], w1_d[0:F, :]),
                             (w3[0:F, :], w3_d[:, :]), (w3[F:P, :], w3_d[:, :]),
                             (bias[:, :], b_d.partition_broadcast(P))):
                sp.dma_start(dst, src).then_inc(weights_in, 16)

            def ring_row(row):
                with sp.Fori(1, NB - 1) as j:
                    load_block(row, wrap(row + 1 + j), block_at(row, j) - 1, COUNTS * row + 1 + 4 * (j - 1))

            ring_row(0)
            load_diag(0)
            with sp.Fori(1, NB) as row:
                load_block(row, wrap(row + 1), block_at(row, 0) - 2, COUNTS * row - 8)
                ring_row(row)
                load_diag(row)

            load_block(NB - 2, NB - 1, PASS2 - 2, COUNTS * NB - 8)
            with sp.Fori(2, NB) as q:
                with sp.Fori(0, q) as j:
                    load_block(NB - 1 - q, NB - 1 - j, block_at2(q, j) - 1)
            load_block(NB - 1, NB - 2, PASS3 - 1)
            with sp.Fori(2, NB) as j:
                load_block(NB - 1, wrap(NB - 1 - j), block_at3(0, j) - 1)
            with sp.Fori(1, NB) as t:
                with sp.Fori(0, NB - t) as j:
                    load_block(NB - 1 - t, wrap(NB - 1 - t - j), block_at3(t, j) - 1)

        @block.tensor
        def _(pe):
            def zero(*parts):
                for hf in range(2):
                    for buf, lo, size in parts:
                        nc.tensor.matmul(buf[lo:lo + size, hf * HALF:(hf + 1) * HALF], zeros[:, 0:size], zeros[:, :],
                                         start=True, stop=False, skip_group_check=True)

            def stream_block(g, tile_of, full, into, early=None):
                both = len(into) == 1
                for pair in range(KT // 2):
                    if pair == 1 and early is not None:
                        early()
                    st = stage[pair // 2]
                    if pair % 2 == 0:
                        pe.wait_ge(staged, 2 * g + pair // 2 + 1)
                    for s in (2 * pair, 2 * pair + 1):
                        full(s)
                        if both:
                            for hf in range(2):
                                mm = nc.tensor.matmul(into[0][:, hf * HALF:(hf + 1) * HALF],
                                                      st[:, (s % 4) * P:(s % 4 + 1) * P],
                                                      tile_of(s)[:, hf * HALF:(hf + 1) * HALF],
                                                      start=False, stop=False, skip_group_check=True)
                            mm.then_inc(ktile_read, 1)
                    if not both:
                        for hf in range(2):
                            for s in (2 * pair, 2 * pair + 1):
                                half = s % 2
                                mm = nc.tensor.matmul(into[half][half * F:(half + 1) * F, hf * HALF:(hf + 1) * HALF],
                                                      st[:, (s % 4) * P:(s % 4) * P + F],
                                                      tile_of(s)[:, hf * HALF:(hf + 1) * HALF],
                                                      start=False, stop=False, skip_group_check=True)
                                if hf == 1:
                                    mm.then_inc(ktile_read, 1)

            def stream_ring(g, n, into, early=None):
                stream_block(g, lambda s: ring[:, s, :],
                             lambda s: pe.wait_ge(ring_full[s], 16 * n + 16), into, early)

            def transposes(tiles):
                for k in range(KT):
                    lo = (k % 2) * F
                    mm = nc.tensor.matmul(turned[lo:lo + F, (k // 2) * P:(k // 2 + 1) * P], tiles(k), ident[:, :],
                                          start=True, stop=True, skip_group_check=True)
                mm.then_inc(turned_done, 1)

            def dense_product(terms, dst):
                for k in range(KT):
                    for i, (lhs, rhs) in enumerate(terms):
                        mm = nc.tensor.matmul(dst[:, k * F:(k + 1) * F], lhs[:, k * P:(k + 1) * P], rhs,
                                              start=(i == 0), stop=(i == len(terms) - 1), skip_group_check=True)
                return mm

            def own_tile(k):
                return act_out[:, k * F:(k + 1) * F]

            def x1_product(row):
                pe.wait_ge(turned_kept, 4 * row + 2)
                pe.wait_ge(count_read, row + 1)
                dense_product([(cat_t[:, :], w0x[:, :]), (agg_t[0:F, :], w0a[:, :])], dense).then_inc(dense_done, 1)

            def own_block(row):
                pe.wait_ge(act_ready, row + 1)
                pe.wait_ge(turned_kept, 4 * row + 2)
                transposes(own_tile)
                pe.wait_ge(own_added, 2 * row + 2)
                for pair in range(KT // 2):
                    for hf in range(2):
                        for half in range(2):
                            k = 2 * pair + half
                            mm = nc.tensor.matmul(own[half * F:(half + 1) * F, hf * HALF:(hf + 1) * HALF], own_tile(k),
                                                  diag[:, k, hf * HALF:(hf + 1) * HALF],
                                                  start=(pair == 0), stop=(pair == KT // 2 - 1), skip_group_check=True)
                mm.then_inc(own_done, 1)
                pe.wait_ge(counted, COUNTS * row + COUNTS)
                for k in range(KT):
                    for half in range(2):
                        lo = half * BLK + k * P
                        mm = nc.tensor.matmul(dense[:, k:k + 1], tally_out[:, lo:lo + P], ones[:, :],
                                              start=(half == 0), stop=(half == 1), skip_group_check=True)
                mm.then_inc(counts_done, 1)

            def diagonal(row):
                stream_block(block_at(row, NB - 1), lambda s: diag[:, s, :],
                             lambda s: pe.wait_ge(diag_full[s // 2], 16 * row + 16), (main, odd))
                pe.wait_ge(turned_kept, 4 * row)
                transposes(lambda k: stage[k // 4][:, (k % 4) * P:(k % 4) * P + F])

            def right_blocks(row, first):
                with pe.Fori(first, NB - 1 - row) as j:
                    stream_ring(block_at(row, j), (NB - 1) * row + j, (main, odd))

            def left_blocks(row, first):
                with pe.Fori(first, row) as col:
                    stream_ring((NB - 1) * row + NB - 1 + col, (NB - 2) * row + NB - 1 + col, (main,))

            def first_products_free(row):
                pe.wait_ge(drained1, 2 * row - 1)
                pe.wait_ge(odd_drained, row)
                zero((main, 0, F), (odd, F, F))

            def second_product_free(row):
                pe.wait_ge(drained1, 2 * row)
                zero((main, F, F))

            pe.wait_ge(const_made, 4)
            zero((main, 0, P), (odd, F, F))
            right_blocks(0, 0)
            diagonal(0)
            pe.wait_ge(weights_in, 8 * 16)
            with pe.Fori(1, NB - 1) as row:
                first_products_free(row)
                stream_ring(block_at(row, 0), (NB - 1) * row, (main, odd), lambda: x1_product(row - 1))
                own_block(row - 1)
                with pe.If(row < NB - 2):
                    right_blocks(row, 1)
                second_product_free(row)
                left_blocks(row, 0)
                diagonal(row)
            first_products_free(NB - 1)
            second_product_free(NB - 1)
            stream_ring(block_at(NB - 1, 0), (NB - 1) * (NB - 1), (main,), lambda: x1_product(NB - 2))
            own_block(NB - 2)
            left_blocks(NB - 1, 1)
            diagonal(NB - 1)
            first_products_free(NB)
            second_product_free(NB)
            x1_product(NB - 1)
            own_block(NB - 1)

            def x2_product(q):
                pe.wait_ge(cat_t_in, q)
                pe.wait_ge(agg2_in, q)
                dense_product([(cat_t[:, :], w1x[:, :])], dense).then_inc(dense_done, 1)

            def h2_transposes(q):
                pe.wait_ge(h2_ready, q)
                pe.wait_ge(turned_kept, 4 * NB + 2 * (q - 1))
                transposes(lambda k: norm_out[:, k * F:(k + 1) * F])

            pe.wait_ge(count_read, NB + 1)
            x2_product(1)
            h2_transposes(1)
            stream_ring(PASS2, PASS2 - NB, (main,))

            def row2(q, into, inner):
                zero((into, 0, P))
                stream_ring(block_at2(q, 0), block_at2(q, 0, NB), (into,), lambda: x2_product(q))
                with inner():
                    with pe.Fori(1, q - 1) as j:
                        stream_ring(block_at2(q, j), block_at2(q, j, NB), (into,))
                h2_transposes(q)
                stream_ring(block_at2(q, q - 1), block_at2(q, q - 1, NB), (into,))

            with pe.Fori(0, NB // 2 - 1) as m:
                row2(2 * m + 2, odd, lambda: pe.If(m > 0))
                row2(2 * m + 3, main, nullcontext)

            def out_product(t):
                pe.wait_ge(cat_t_in, NB + 1 + t)
                pe.wait_ge(drained3, t + 1)
                pe.wait_ge(agg3_in, t + 1)
                pe.wait_ge(out_step, 4 * t + 4)
                dense_product([(cat_t[0:F, :], w3[0:F, :])], dense)
                dense_product([(agg_t[:, :], w3[:, :])], turned).then_inc(dense_done, 1)

            zero((own, 0, P))
            stream_block(PASS3, lambda s: diag[:, s, :], lambda s: None, (own, own), lambda: x2_product(NB))
            with pe.Fori(1, NB) as j:
                stream_ring(block_at3(0, j), block_at3(0, j, NB + 1), (own, own))
            h2_transposes(NB)
            pe.wait_ge(turned_kept, 6 * NB)
            with pe.Fori(1, NB) as t:
                pe.wait_ge(drained3, t)
                pe.wait_ge(agg3_in, t)
                zero((main, 0, F), (odd, F, F))
                out_product(t - 1)
                with pe.Fori(0, NB - t) as j:
                    stream_ring(block_at3(t, j), block_at3(t, j, NB + 1), (main, odd))
            out_product(NB - 1)

        @block.scalar
        def _(act):
            def stage_block(g, col, free=True, width=2 * F):
                src = cat[:, bass.ds(col * KT * 2 * F, KT * 2 * F)].rearrange("p (k c) -> p k c", c=2 * F)
                for h in range(2):
                    if free:
                        act.wait_ge(ktile_read, KT * (g - 1) + 4 * (h + 1))
                    dst = stage[h][:, :].rearrange("p (k c) -> p k c", c=2 * F)
                    nc.scalar.copy(dst[:, :, 0:width], src[:, 4 * h:4 * h + 4, 0:width]).then_inc(staged, 1)

            def tanh_rows(done):
                act.wait_ge(dense_done, done)
                nc.scalar.activation(act_out[:, :], dense[:, :], ACT.Tanh).then_inc(act_ready, 1)

            def keep_x1(row):
                act.wait_ge(act_ready, row + 1)
                nc.scalar.copy(cat_of(row, 1), by_tile(act_out)).then_inc(x1_kept, 1)

            def keep_turned(count, dst):
                act.wait_ge(turned_done, count)
                tiles = dst.rearrange("p (m two c) -> p two m c", two=2, c=P)
                for half in range(2):
                    src = turned[half * F:(half + 1) * F, :].rearrange("p (m c) -> p m c", c=P)
                    nc.scalar.copy(tiles[:, half], src).then_inc(turned_kept, 1)

            def drain_first(row):
                act.wait_ge(ktile_read, KT * NB * row + KT * NB)
                nc.scalar.copy(agg_t[0:F, :], main[0:F, :]).then_inc(drained1, 1)

            def drain_second(row):
                nc.scalar.copy(rows_of(feat, F, P, row), main[F:P, :]).then_inc(drained1, 1)

            act.wait_ge(cat_cleared, 1)
            act.wait_ge(h_ready, 1)
            stage_block(0, 1, free=False)
            with act.Fori(1, NB - 1) as j:
                act.wait_ge(h_ready, j + 1)
                stage_block(block_at(0, j), j + 1)
            act.wait_ge(h_ready, NB)
            stage_block(block_at(0, NB - 1), 0)
            keep_turned(1, cat_t[0:F, :])
            drain_first(0)
            with act.Fori(1, NB) as row:
                act.wait_ge(turned_done, 2 * row - 1)
                stage_block(block_at(row, 0), wrap(row + 1))
                drain_second(row - 1)
                tanh_rows(row)
                keep_x1(row - 1)
                act.wait_ge(x1_kept, row)
                with act.Fori(1, NB - 1) as j:
                    stage_block(block_at(row, j), wrap(row + 1 + j))
                stage_block(block_at(row, NB - 1), row)
                keep_turned(2 * row, rows_of(feat, 0, F, row - 1))
                keep_turned(2 * row + 1, cat_t[0:F, :])
                drain_first(row)
            drain_second(NB - 1)
            tanh_rows(NB)
            keep_x1(NB - 1)
            keep_turned(2 * NB, rows_of(feat, 0, F, NB - 1))

            def bring_features(value, row):
                act.wait_ge(dense_done, value)
                nc.scalar.copy(cat_t[0:F, :], rows_of(feat, 0, F, row)).then_inc(cat_t_in, 1)

            def keep_part(q):
                act.wait_ge(drained2, q - 1)
                act.wait_ge(agg2_in, q)
                nc.scalar.copy(rows_of(feat, F, P, NB - q), agg_t[F:P, :]).then_inc(part_kept, 1)

            def keep_h2(q):
                act.wait_ge(h2_ready, q)
                nc.scalar.copy(cat_of(NB - q, 0), by_tile(norm_out)).then_inc(h2_kept, 1)
                act.wait_ge(h2_kept, q)

            act.wait_ge(turned_kept, 4 * NB)
            act.wait_ge(x1_kept, NB)
            bring_features(NB, NB - 1)
            act.wait_ge(own_done, NB)
            tanh_rows(NB + 1)
            keep_h2(1)
            act.wait_ge(turned_done, 2 * NB - 1)
            stage_block(PASS2, NB - 1)
            keep_turned(2 * NB + 1, rows_of(feat, 0, F, NB - 1))
            bring_features(NB + 1, NB - 2)

            def drain_partial(q, buf):
                act.wait_ge(ktile_read, KT * block_at2(q + 1, 0))
                nc.scalar.copy(agg_t[F:P, :], buf[0:F, :]).then_inc(drained2, 1)

            stage_block(block_at2(2, 0), NB - 1)
            drain_partial(1, main)

            def row2(q, buf, inner):
                act.wait_ge(y_ready, q - 1)
                tanh_rows(NB + q)
                keep_part(q)
                with inner():
                    with act.Fori(1, q - 1) as j:
                        stage_block(block_at2(q, j), NB - 1 - j)
                keep_h2(q)
                stage_block(block_at2(q, q - 1), wrap(NB - q))
                keep_turned(2 * NB + q, rows_of(feat, 0, F, NB - q))
                bring_features(NB + q, NB - 1 - q)
                stage_block(block_at2(q + 1, 0), NB - 1)
                act.wait_ge(part_kept, q - 1)
                drain_partial(q, buf)

            with act.Fori(0, NB // 2 - 1) as m:
                row2(2 * m + 2, odd, lambda: act.If(m > 0))
                row2(2 * m + 3, main, nullcontext)

            def drain_even(t, buf):
                act.wait_ge(ktile_read, KT * block_at3(t + 1, 0))
                nc.scalar.copy(agg_t[0:F, :], buf[0:F, :]).then_inc(drained3, 1)

            act.wait_ge(y_ready, NB - 1)
            tanh_rows(2 * NB)
            keep_part(NB)
            with act.Fori(1, NB - 1) as j:
                stage_block(block_at3(0, j), NB - 1 - j, width=F)
            keep_h2(NB)
            stage_block(block_at3(0, NB - 1), 0, width=F)
            keep_turned(3 * NB, rows_of(feat, 0, F, 0))
            bring_features(2 * NB, NB - 1)
            drain_even(0, own)
            act.wait_ge(turned_kept, 6 * NB)
            with act.Fori(1, NB) as t:
                with act.Fori(0, NB - t) as j:
                    stage_block(block_at3(t, j), wrap(NB - 1 - t - j), width=F)
                bring_features(2 * NB + t, NB - 1 - t)
                drain_even(t, main)

        @block.vector
        def _(dve):
            def norm_first(i, src):
                def after(k):
                    dve.wait_ge(norm_step, 6 * i + k)

                nc.vector.tensor_reduce(total[:, :], src, AX.X, ALU.add).then_inc(norm_step, 1)
                after(1)
                nc.vector.tensor_scalar(negmean[:, :], total[:, :], -1.0 / F, None, ALU.mult).then_inc(norm_step, 1)
                after(2)
                nc.vector.tensor_tensor(by_tile(centred), src, spread(negmean[:, :]), ALU.add).then_inc(norm_step, 1)
                after(3)
                nc.vector.tensor_tensor(by_tile(square), by_tile(centred), by_tile(centred), ALU.mult).then_inc(norm_step, 1)
                after(4)
                nc.vector.tensor_reduce(sqsum[:, :], by_tile(square), AX.X, ALU.add).then_inc(norm_step, 1)
                after(5)
                nc.vector.tensor_scalar(var[:, :], sqsum[:, :], 1.0 / F, EPS, ALU.mult, ALU.add).then_inc(norm_step, 1)

            def norm_last(i, dst):
                dve.wait_ge(rstd_ready, i + 1)
                return nc.vector.scalar_tensor_tensor(out=dst, in0=by_tile(centred), scalar=0.0,
                                                      in1=spread(rstd[:, :]), op0=ALU.max, op1=ALU.mult)

            def count(done, dst, tiles):
                dve.wait_ge(counted, done)
                nc.vector.scalar_tensor_tensor(out=dst[:, :], in0=tiles.rearrange("p s r -> p (s r)"), scalar=0.0,
                                               in1=tally[:, :], op0=ALU.not_equal, op1=ALU.add).then_inc(counted, 1)

            def count_ring(row, j):
                for c in range(KT // 2):
                    for s in (2 * c, 2 * c + 1):
                        dve.wait_ge(ring_full[s], 16 * ((NB - 1) * row + j) + 16)
                    count(COUNTS * row + 1 + 4 * j + c, tally, ring[:, 2 * c:2 * c + 2, :])

            def count_diag(row):
                for c in range(KT // 2):
                    dve.wait_ge(diag_full[c], 16 * row + 16)
                    dst = tally if c < KT // 2 - 1 else tally_out
                    count(COUNTS * row + 1 + 4 * (NB - 1) + c, dst, diag[:, 2 * c:2 * c + 2, :])

            def take_counts(row):
                dve.wait_ge(counts_done, row + 1)
                nc.vector.tensor_copy(degree[:, bass.ds(row * KT, KT)], dense[:, 0:KT]).then_inc(count_read, 1)

            def add_own(row):
                dve.wait_ge(own_done, row + 1)
                dve.wait_ge(drained1, 2 * row + 2)
                part = rows_of(feat, F, P, row)
                nc.vector.tensor_tensor(part, part, own[F:P, :], ALU.add).then_inc(own_added, 1)
                dve.wait_ge(own_added, 2 * row + 3)
                nc.vector.tensor_tensor(part, part, own[0:F, :], ALU.add).then_inc(own_added, 1)

            def drain_odd(row):
                dve.wait_ge(ktile_read, KT * NB * row + KT * NB)
                nc.vector.tensor_copy(cat_t[F:P, :], odd[F:P, :]).then_inc(odd_drained, 1)

            dve.sem_inc(count_read, 1)
            dve.sem_inc(own_added, 2)
            dve.sem_inc(out_step, 4)

            def x_first(i, g):
                dve.wait_ge(x_in[g], 16)
                norm_first(i, nodes_of(xres, g))

            nc.vector.memset(cat[:, :].rearrange("p (k c) -> p k c", c=2 * F)[:, :, F:2 * F], 0.0).then_inc(cat_cleared, 1)
            x_first(0, 1)
            nc.vector.memset(tally[:, :], 0.0).then_inc(counted, 1)
            norm_last(0, cat_of(1, 0)).then_inc(h_ready, 1)
            for j in range(NB - 1):
                x_first(j + 1, (j + 2) % NB)
                count_ring(0, j)
                norm_last(j + 1, cat_of((j + 2) % NB, 0)).then_inc(h_ready, 1)
            count_diag(0)
            drain_odd(0)
            with dve.Fori(1, NB) as row:
                dve.wait_ge(counted, COUNTS * row)
                nc.vector.memset(tally[:, :], 0.0).then_inc(counted, 1)
                with dve.Fori(0, NB - 1) as j:
                    count_ring(row, j)
                dve.wait_ge(counts_done, row)
                count_diag(row)
                take_counts(row - 1)
                add_own(row - 1)
                drain_odd(row)
            take_counts(NB - 1)
            add_own(NB - 1)

            def y_and_norm(q, row):
                y = nodes_of(xres, row)
                dve.wait_ge(act_ready, NB + q)
                nc.vector.tensor_tensor(y, y, by_tile(act_out), ALU.add).then_inc(y_ready, 1)
                dve.wait_ge(y_ready, q)
                norm_first(NB + q - 1, nodes_of(xres, wrap(row)))

            def h2_rows(q):
                norm_last(NB + q - 1, by_tile(norm_out)).then_inc(h2_ready, 1)

            dve.wait_ge(own_added, 2 * NB + 2)
            dve.wait_ge(dense_done, NB)
            nc.vector.tensor_copy(cat_t[F:P, :], rows_of(feat, F, P, NB - 1)).then_inc(agg2_in, 1)
            dve.wait_ge(agg2_in, 1)
            nc.vector.memset(rows_of(feat, F, P, NB - 1), 0.0).then_inc(part_cleared, 1)
            y_and_norm(1, NB - 1)
            h2_rows(1)
            dve.wait_ge(count_read, NB + 1)
            nc.vector.tensor_scalar(degree1[:, :], degree[:, :], 1.0, None, ALU.max).then_inc(degree_ready, 1)

            def row2(q, before):
                row = settled(dve, NB - q)
                dve.wait_ge(ktile_read, KT * block_at2(q, 0))
                dve.wait_ge(dense_done, NB + q - 1)
                nc.vector.tensor_tensor(cat_t[F:P, :], rows_of(feat, F, P, row), before[F:P, :],
                                        ALU.add).then_inc(agg2_in, 1)
                y_and_norm(q, row)
                dve.wait_ge(h2_kept, q - 1)
                dve.wait_ge(turned_done, 2 * NB + q - 1)
                h2_rows(q)

            with dve.Fori(0, NB // 2 - 1) as m:
                row2(2 * m + 2, main)
                row2(2 * m + 3, odd)
            row2(NB, main)
            dve.wait_ge(invroot_ready, 1)
            nc.vector.tensor_scalar(neg_invroot[:, :], invroot[:, :], -1.0, None, ALU.mult).then_inc(degree_ready, 1)
            dve.wait_ge(part_cleared, 1)
            dve.wait_ge(degree_ready, 2)

            def row3(t, buf):
                row = settled(dve, NB - 1 - t)
                dve.wait_ge(ktile_read, KT * block_at3(t + 1, 0))
                dve.wait_ge(part_kept, NB - 1)
                dve.wait_ge(dense_done, 2 * NB + t)
                nc.vector.tensor_tensor(agg_t[F:P, :], rows_of(feat, F, P, row), buf[F:P, :],
                                        ALU.add).then_inc(agg3_in, 1)
                dve.wait_ge(dense_done, 2 * NB + 1 + t)
                scale = neg_invroot[:, bass.ds(row * KT, KT)].unsqueeze(2).to_broadcast([P, KT, F])
                nc.vector.tensor_tensor(by_tile(square), by_tile(turned), scale, ALU.mult).then_inc(out_step, 1)
                dve.wait_ge(out_step, 4 * t + 5)
                nc.vector.tensor_tensor(centred[:, :], square[:, :], dense[:, :], ALU.add).then_inc(out_step, 1)
                dve.wait_ge(out_step, 4 * t + 6)
                nc.vector.tensor_tensor(by_tile(square), by_tile(centred),
                                        bias[:, :].unsqueeze(1).to_broadcast([P, KT, F]), ALU.add).then_inc(out_step, 1)
                dve.wait_ge(out_step, 4 * t + 7)
                y = nodes_of(xres, row)
                nc.vector.scalar_tensor_tensor(out=y, in0=by_tile(square), scalar=0.0, in1=y,
                                               op0=ALU.max, op1=ALU.add).then_inc(out_step, 1)

            row3(0, own)
            with dve.Fori(1, NB) as t:
                row3(t, odd)

        @block.gpsimd
        def _(pool):
            nc.gpsimd.memset(ident[:, :], 0.0).then_inc(const_made, 1)
            nc.gpsimd.memset(zeros[:, :], 0.0).then_inc(const_made, 1)
            nc.gpsimd.memset(ones[:, :], 1.0).then_inc(const_made, 1)
            pool.wait_ge(const_made, 3)
            nc.gpsimd.affine_select(out=ident[:, :], in_=ident[:, :], compare_op=ALU.not_equal, fill=1.0, base=0,
                                    pattern=[[-1, P]], channel_multiplier=1).then_inc(const_made, 1)
            nc.gpsimd.memset(minus_half[:, :], -0.5).then_inc(const_made, 1)
            pool.wait_ge(const_made, 5)

            def power(i):
                pool.wait_ge(norm_step, 6 * i + 6)
                nc.gpsimd.tensor_tensor(rstd[:, :], var[:, :], minus_half[:, 0:KT], ALU.pow).then_inc(rstd_ready, 1)

            with pool.Fori(0, NB + 1) as i:
                power(i)
            pool.wait_ge(degree_ready, 1)
            nc.gpsimd.tensor_tensor(invroot[:, :], degree1[:, :], minus_half[:, :], ALU.pow).then_inc(invroot_ready, 1)
            with pool.Fori(NB + 1, 2 * NB) as i:
                power(i)
            with pool.Fori(0, NB) as t:
                first = settled(pool, (NB - 1 - t) * GW)
                pool.wait_ge(out_step, 4 * t + 8)
                rows = bass.ds(first, GW)
                pool.dma_start(out_d[:, rows], xres[:, rows]).then_inc(out_stored, 16)
            pool.wait_ge(out_stored, 16 * NB)


def kernel(**inputs):
    import numpy as np
    import concourse.bacc as bacc
    from concourse.bass_utils import run_bass_kernel_spmd

    n, f = inputs["x"].shape
    nb = n // BLK

    def node_major(a):
        return np.ascontiguousarray(a.reshape(n // P, P, f).transpose(1, 0, 2).reshape(P, -1))

    adj = np.asarray(inputs["adj"]).reshape(nb, BLK, nb, KT, P)
    arrays = {
        "x": node_major(np.asarray(inputs["x"])),
        "adj": np.ascontiguousarray(adj.transpose(0, 2, 3, 4, 1)).reshape(nb * nb * KT, P, BLK),
        "w0": np.ascontiguousarray(inputs["L0_gnn_W"][0]),
        "w1": np.ascontiguousarray(inputs["L0_gnn_W"][1]),
        "w3": np.ascontiguousarray(inputs["L1_gnn_W"]),
        "b": np.ascontiguousarray(inputs["L1_gnn_b"]),
    }
    nc = bacc.Bacc("TRN2", target_bir_lowering=False, num_devices=1)
    args = [nc.dram_tensor("in_" + name, a.shape, mybir.dt.from_np(a.dtype), kind="ExternalInput").ap()
            for name, a in arrays.items()]
    out = nc.dram_tensor("out", (P, n // P * f), F32, kind="ExternalOutput").ap()
    gnn_program(nc, *args, out)
    r = run_bass_kernel_spmd(nc, [{"in_" + name: a for name, a in arrays.items()}], core_ids=[0])
    return r.results[0]["out"].reshape(P, n // P, f).transpose(1, 0, 2).reshape(n, f)
```

```python
import concourse.bass as bass
from concourse import mybir
from contextlib import ExitStack, nullcontext

F32 = mybir.dt.float32
BF16 = mybir.dt.bfloat16
ALU = mybir.AluOpType
ACT = mybir.ActivationFunctionType
AX = mybir.AxisListType

P = 128
F = 64
BLK = 1024
KT = BLK // P
HALF = 512
EPS = 1e-5


def gnn_program(nc, x_d, adj_d, w0_d, w1_d, w3_d, b_d, out_d):
    NB = x_d.shape[1] // (KT * F)
    GW = KT * F
    COUNTS = 4 * NB + 1
    PASS2 = NB * NB
    PASS3 = PASS2 + NB * (NB - 1) // 2

    def block_at(row, j):
        return NB * row + j

    def block_at2(q, j, skipped=0):
        return PASS2 - skipped + ((q * (q - 1)) >> 1) + j

    def block_at3(t, j, skipped=0):
        before = (t * (2 * NB + 1 - t)) >> 1
        if not isinstance(t, int):
            before = before & (NB * NB - 1)
        return PASS3 - skipped + before + j

    def wrap(i):
        return i & (NB - 1)

    def settled(eng, value):
        return value if isinstance(value, int) else eng.snap(eng.to_reg(value))

    ctx = ExitStack()
    with ctx:
        def sb(name, shape, dt=F32):
            return ctx.enter_context(nc.sbuf_tensor(name, shape, dt))

        def pb(name, shape):
            return ctx.enter_context(nc.psum_tensor(name, shape, F32))

        def sem(name):
            return ctx.enter_context(nc.semaphore(name))

        ring = sb("ring", [P, KT, BLK])
        diag = sb("diag", [P, KT, BLK])
        ahead = sb("ahead", [P, KT, BLK])
        cat = sb("cat", [P, NB * KT * 2 * F])
        feat = sb("feat", [P, NB * BLK])
        xres = sb("xres", [P, NB * GW])
        stage = [sb(f"stage{h}", [P, 4 * 2 * F]) for h in range(2)]
        act_t = sb("act_t", [P, HALF])
        node_out = sb("node_out", [P, GW])
        cat_t = sb("cat_t", [P, BLK])
        agg_t = sb("agg_t", [P, BLK])
        centred = sb("centred", [P, GW])
        square = sb("square", [P, GW])
        total = sb("total", [P, KT])
        negmean = sb("negmean", [P, KT])
        sqsum = sb("sqsum", [P, KT])
        var = sb("var", [P, KT])
        rstd = sb("rstd", [P, KT])
        tally = sb("tally", [P, 2 * BLK], BF16)
        tally_out = sb("tally_out", [P, 2 * BLK], BF16)
        degree = sb("degree", [P, NB * KT])
        minus_half = sb("minus_half", [P, NB * KT])
        w0x = sb("w0x", [P, F])
        w0a = sb("w0a", [F, F])
        w1x = sb("w1x", [P, F])
        w3 = sb("w3", [P, F])
        bias = sb("bias", [P, F])
        ident = sb("ident", [P, P])
        zeros = sb("zeros", [P, HALF], BF16)
        ones = sb("ones", [P, 1], BF16)

        main = pb("main", [P, BLK])
        odd = pb("odd", [P, BLK])
        own = pb("own", [P, BLK])
        dense = pb("dense", [P, HALF])
        turned = pb("turned", [P, HALF])

        ring_full = [sem(f"ring_full{s}") for s in range(KT)]
        diag_full = [sem(f"diag_full{c}") for c in range(KT // 2)]
        ahead_full = [sem(f"ahead_full{c}") for c in range(KT // 2)]
        x_in = [sem(f"x_in{g}") for g in range(NB)]
        weights_in = sem("weights_in")
        out_stored = sem("out_stored")
        const_made = sem("const_made")
        cat_cleared = sem("cat_cleared")
        ktile_read = sem("ktile_read")
        dense_done = sem("dense_done")
        turned_done = sem("turned_done")
        own_done = sem("own_done")
        counts_done = sem("counts_done")
        staged = sem("staged")
        act_ready = sem("act_ready")
        x1_ready = sem("x1_ready")
        x1_kept = sem("x1_kept")
        turned_kept = sem("turned_kept")
        x1t_kept = sem("x1t_kept")
        drained1 = sem("drained1")
        cat_t_in = sem("cat_t_in")
        drained2 = sem("drained2")
        part_kept = sem("part_kept")
        h2_kept = sem("h2_kept")
        drained3 = sem("drained3")
        h_ready = sem("h_ready")
        norm_step = sem("norm_step")
        counted = sem("counted")
        count_read = sem("count_read")
        odd_drained = sem("odd_drained")
        own_added = sem("own_added")
        part_cleared = sem("part_cleared")
        agg2_in = sem("agg2_in")
        y_ready = sem("y_ready")
        h2_ready = sem("h2_ready")
        degree_ready = sem("degree_ready")
        agg3_in = sem("agg3_in")
        out_step = sem("out_step")
        rstd_ready = sem("rstd_ready")
        invroot_ready = sem("invroot_ready")

        block = ctx.enter_context(nc.Block())

        def rows_of(buf, lo, hi, r):
            return buf[lo:hi, bass.ds(r * BLK, BLK)]

        def nodes_of(buf, r):
            return buf[:, bass.ds(r * GW, GW)].rearrange("p (k c) -> p k c", c=F)

        def cat_of(r, half):
            v = cat[:, bass.ds(r * KT * 2 * F, KT * 2 * F)].rearrange("p (k c) -> p k c", c=2 * F)
            return v[:, :, half * F:(half + 1) * F]

        def by_tile(buf):
            return buf[:, :].rearrange("p (k c) -> p k c", c=F)

        def spread(small):
            return small.unsqueeze(2).to_broadcast([P, KT, F])

        @block.sync
        def _(sp):
            def load(tile, s):
                sp.dma_start(ring[:, s, :], adj_d[tile]).then_inc(ring_full[s], 16)

            def load_block(row, col, block, steps=None):
                tile0, read0 = settled(sp, (row * NB + col) * KT), settled(sp, KT * block)
                for s in range(KT):
                    tile, read = settled(sp, tile0 + s), settled(sp, read0 + s + 1)
                    if steps is not None:
                        seen = settled(sp, steps + s // 2 + 1)
                        sp.wait_ge(counted, seen)
                    sp.wait_ge(ktile_read, read)
                    load(tile, s)

            def load_pairs(dst, first, full):
                for c in range(KT // 2):
                    src = adj_d[bass.ds(first + 2 * c, 2)]
                    sp.dma_start(dst[:, 2 * c:2 * c + 2, :], src.rearrange("s p r -> p s r")).then_inc(full[c], 16)

            def load_diag(row):
                first = row * (NB + 1) * KT
                if not isinstance(row, int):
                    first, free, seen = settled(sp, first), settled(sp, row), settled(sp, COUNTS * row)
                    sp.wait_ge(own_done, free)
                    sp.wait_ge(counted, seen)
                load_pairs(diag, first, diag_full)

            def load_x(g):
                sp.dma_start(xres[:, g * GW:(g + 1) * GW], x_d[:, g * GW:(g + 1) * GW]).then_inc(x_in[g], 16)

            load_x(1)
            load_x(2 % NB)
            for s in range(KT):
                load(KT + s, s)
                if s < NB - 2:
                    load_x((s + 3) % NB)
            for dst, src in ((w0x[0:F, :], w0_d[F:2 * F, :]), (w0x[F:P, :], w0_d[0:F, :]), (w0a[:, :], w0_d[0:F, :]),
                             (w1x[0:F, :], w1_d[F:2 * F, :]), (w1x[F:P, :], w1_d[0:F, :]),
                             (w3[0:F, :], w3_d[:, :]), (w3[F:P, :], w3_d[:, :]),
                             (bias[:, :], b_d.partition_broadcast(P))):
                sp.dma_start(dst, src).then_inc(weights_in, 16)

            def ring_row(row):
                with sp.Fori(1, NB - 1) as j:
                    load_block(row, wrap(row + 1 + j), block_at(row, j) - 1, COUNTS * row + 1 + 4 * (j - 1))

            ring_row(0)
            load_diag(0)
            with sp.Fori(1, NB) as row:
                load_block(row, wrap(row + 1), block_at(row, 0) - 2, COUNTS * row - 8)
                ring_row(row)
                load_diag(row)

            load_block(NB - 2, NB - 1, PASS2 - 2, COUNTS * NB - 8)
            load_pairs(ahead, ((NB - 1) * NB + NB - 2) * KT, ahead_full)
            with sp.Fori(2, NB) as q:
                with sp.Fori(0, q) as j:
                    load_block(NB - 1 - q, NB - 1 - j, block_at2(q, j) - 1)
            load_block(NB - 1, NB - 3, PASS3 - 1)
            with sp.Fori(3, NB) as j:
                load_block(NB - 1, wrap(NB - 1 - j), block_at3(0, j) - 1)
            with sp.Fori(1, NB) as t:
                with sp.Fori(0, NB - t) as j:
                    load_block(NB - 1 - t, wrap(NB - 1 - t - j), block_at3(t, j) - 1)

        @block.tensor
        def _(pe):
            def zero(*parts):
                for hf in range(2):
                    for buf, lo, size in parts:
                        nc.tensor.matmul(buf[lo:lo + size, hf * HALF:(hf + 1) * HALF], zeros[:, 0:size], zeros[:, :],
                                         start=True, stop=False, skip_group_check=True)

            def stream_block(g, tile_of, full, into, between={}):
                both = len(into) == 1
                for pair in range(KT // 2):
                    if pair in between:
                        between[pair]()
                    st = stage[pair // 2]
                    if pair % 2 == 0:
                        pe.wait_ge(staged, 2 * g + pair // 2 + 1)
                    for s in (2 * pair, 2 * pair + 1):
                        full(s)
                        if both:
                            for hf in range(2):
                                mm = nc.tensor.matmul(into[0][:, hf * HALF:(hf + 1) * HALF],
                                                      st[:, (s % 4) * P:(s % 4 + 1) * P],
                                                      tile_of(s)[:, hf * HALF:(hf + 1) * HALF],
                                                      start=False, stop=False, skip_group_check=True)
                            mm.then_inc(ktile_read, 1)
                    if not both:
                        for hf in range(2):
                            for s in (2 * pair, 2 * pair + 1):
                                half = s % 2
                                mm = nc.tensor.matmul(into[half][half * F:(half + 1) * F, hf * HALF:(hf + 1) * HALF],
                                                      st[:, (s % 4) * P:(s % 4) * P + F],
                                                      tile_of(s)[:, hf * HALF:(hf + 1) * HALF],
                                                      start=False, stop=False, skip_group_check=True)
                                if hf == 1:
                                    mm.then_inc(ktile_read, 1)

            def stream_ring(g, n, into, between={}):
                stream_block(g, lambda s: ring[:, s, :],
                             lambda s: pe.wait_ge(ring_full[s], 16 * n + 16), into, between)

            def turn_pairs(buf):
                for c in range(KT // 2):
                    mm = nc.tensor.transpose(turned[:, c * P:(c + 1) * P], buf[:, c * P:(c + 1) * P], ident[:, :])
                mm.then_inc(turned_done, 1)

            def product_t(terms):
                for i, (weights, operand) in enumerate(terms):
                    for hf in range(2):
                        mm = nc.tensor.matmul(dense[hf * F:(hf + 1) * F, :], weights, operand[:, hf * HALF:(hf + 1) * HALF],
                                              start=(i == 0), stop=(i == len(terms) - 1), skip_group_check=True)
                mm.then_inc(dense_done, 1)

            def x1_product(row):
                pe.wait_ge(turned_kept, 2 * row + 2)
                pe.wait_ge(count_read, row + 1)
                product_t([(w0x[:, :], cat_t[:, :]), (w0a[:, :], agg_t[0:F, :])])

            def x1_turn(row):
                pe.wait_ge(act_ready, row + 1)
                turn_pairs(act_t)

            def own_part(row, part):
                if part == 0:
                    pe.wait_ge(x1_ready, row + 1)
                    pe.wait_ge(own_added, 2 * row + 2)
                for pair in (2 * part, 2 * part + 1):
                    for hf in range(2):
                        for half in range(2):
                            k = 2 * pair + half
                            mm = nc.tensor.matmul(own[half * F:(half + 1) * F, hf * HALF:(hf + 1) * HALF],
                                                  node_out[:, k * F:(k + 1) * F], diag[:, k, hf * HALF:(hf + 1) * HALF],
                                                  start=(pair == 0), stop=(pair == KT // 2 - 1), skip_group_check=True)
                if part == 1:
                    mm.then_inc(own_done, 1)

            def counts(row):
                pe.wait_ge(counted, COUNTS * row + COUNTS)
                for k in range(KT):
                    for half in range(2):
                        lo = half * BLK + k * P
                        mm = nc.tensor.matmul(dense[:, k:k + 1], tally_out[:, lo:lo + P], ones[:, :],
                                              start=(half == 0), stop=(half == 1), skip_group_check=True)
                mm.then_inc(counts_done, 1)

            def diagonal(row):
                stream_block(block_at(row, NB - 1), lambda s: diag[:, s, :],
                             lambda s: pe.wait_ge(diag_full[s // 2], 16 * row + 16), (main, odd))
                if not isinstance(row, int) or row > 0:
                    pe.wait_ge(x1_ready, row)
                for k in range(KT):
                    lo = (k % 2) * F
                    mm = nc.tensor.matmul(turned[lo:lo + F, (k // 2) * P:(k // 2 + 1) * P],
                                          stage[k // 4][:, (k % 4) * P:(k % 4) * P + F], ident[:, :],
                                          start=True, stop=True, skip_group_check=True)
                mm.then_inc(turned_done, 1)

            def right_blocks(row, first):
                with pe.Fori(first, NB - 1 - row) as j:
                    stream_ring(block_at(row, j), (NB - 1) * row + j, (main, odd))

            def left_blocks(row, first):
                with pe.Fori(first, row) as col:
                    stream_ring((NB - 1) * row + NB - 1 + col, (NB - 2) * row + NB - 1 + col, (main,))

            def first_products_free(row):
                pe.wait_ge(drained1, 2 * row - 1)
                pe.wait_ge(odd_drained, row)
                zero((main, 0, F), (odd, F, F))

            def second_product_free(row):
                pe.wait_ge(drained1, 2 * row)
                zero((main, F, F))

            pe.wait_ge(const_made, 4)
            zero((main, 0, P), (odd, F, F))
            right_blocks(0, 0)
            diagonal(0)
            pe.wait_ge(weights_in, 8 * 16)
            with pe.Fori(1, NB - 1) as row:
                first_products_free(row)
                stream_ring(block_at(row, 0), (NB - 1) * row, (main, odd),
                            {1: lambda: x1_product(row - 1), 3: lambda: x1_turn(row - 1)})
                own_part(row - 1, 0)
                with pe.If(row < NB - 2):
                    stream_ring(block_at(row, 1), (NB - 1) * row + 1, (main, odd))
                own_part(row - 1, 1)
                counts(row - 1)
                with pe.If(row < NB - 3):
                    right_blocks(row, 2)
                second_product_free(row)
                left_blocks(row, 0)
                diagonal(row)
            first_products_free(NB - 1)
            second_product_free(NB - 1)
            stream_ring(block_at(NB - 1, 0), (NB - 1) * (NB - 1), (main,),
                        {1: lambda: x1_product(NB - 2), 2: lambda: x1_turn(NB - 2)})
            own_part(NB - 2, 0)
            own_part(NB - 2, 1)
            counts(NB - 2)
            left_blocks(NB - 1, 1)
            diagonal(NB - 1)
            first_products_free(NB)
            second_product_free(NB)
            x1_product(NB - 1)
            x1_turn(NB - 1)
            own_part(NB - 1, 0)
            own_part(NB - 1, 1)
            counts(NB - 1)

            def x2_product(q):
                pe.wait_ge(cat_t_in, q)
                pe.wait_ge(agg2_in, q)
                product_t([(w1x[:, :], cat_t[:, :])])

            def x2_turn(q):
                pe.wait_ge(act_ready, NB + q)
                pe.wait_ge(turned_kept, 2 * NB + 2 * (q - 1))
                turn_pairs(act_t)

            def h2_turn(q):
                pe.wait_ge(h2_ready, q)
                turn_pairs(node_out)

            pe.wait_ge(count_read, NB + 1)
            x2_product(1)
            x2_turn(1)
            h2_turn(1)
            stream_ring(PASS2, PASS2 - NB, (main,))

            def row2(q, into, inner):
                zero((into, 0, P))
                stream_ring(block_at2(q, 0), block_at2(q, 0, NB), (into,),
                            {1: lambda: x2_product(q), 2: lambda: x2_turn(q)})
                with inner():
                    with pe.Fori(1, q - 1) as j:
                        stream_ring(block_at2(q, j), block_at2(q, j, NB), (into,))
                h2_turn(q)
                stream_ring(block_at2(q, q - 1), block_at2(q, q - 1, NB), (into,))

            with pe.Fori(0, NB // 2 - 1) as m:
                row2(2 * m + 2, odd, lambda: pe.If(m > 0))
                row2(2 * m + 3, main, nullcontext)

            def dense_product(operand, weights, dst):
                for k in range(KT):
                    mm = nc.tensor.matmul(dst[:, k * F:(k + 1) * F], operand[:, k * P:(k + 1) * P], weights,
                                          start=True, stop=True, skip_group_check=True)
                return mm

            def out_product(t):
                pe.wait_ge(cat_t_in, NB + 1 + t)
                pe.wait_ge(drained3, t + 1)
                pe.wait_ge(agg3_in, t + 1)
                pe.wait_ge(out_step, 4 * t + 4)
                dense_product(cat_t[0:F, :], w3[0:F, :], dense)
                dense_product(agg_t[:, :], w3[:, :], turned).then_inc(dense_done, 1)

            zero((own, 0, P))
            stream_block(PASS3, lambda s: diag[:, s, :], lambda s: None, (own, own),
                         {1: lambda: x2_product(NB), 2: lambda: x2_turn(NB)})
            stream_block(PASS3 + 1, lambda s: ahead[:, s, :], lambda s: pe.wait_ge(ahead_full[s // 2], 16), (own, own))
            with pe.Fori(2, NB) as j:
                stream_ring(block_at3(0, j), block_at3(0, j, NB + 2), (own, own))
            h2_turn(NB)
            pe.wait_ge(turned_kept, 4 * NB)
            with pe.Fori(1, NB) as t:
                pe.wait_ge(drained3, t)
                pe.wait_ge(agg3_in, t)
                zero((main, 0, F), (odd, F, F))
                stream_ring(block_at3(t, 0), block_at3(t, 0, NB + 2), (main, odd), {1: lambda: out_product(t - 1)})
                with pe.If(t < NB - 1):
                    with pe.Fori(1, NB - t) as j:
                        stream_ring(block_at3(t, j), block_at3(t, j, NB + 2), (main, odd))
            out_product(NB - 1)

        @block.scalar
        def _(act):
            def stage_block(g, col, free=True, width=2 * F):
                src = cat[:, bass.ds(col * KT * 2 * F, KT * 2 * F)].rearrange("p (k c) -> p k c", c=2 * F)
                for h in range(2):
                    if free:
                        act.wait_ge(ktile_read, KT * (g - 1) + 4 * (h + 1))
                    dst = stage[h][:, :].rearrange("p (k c) -> p k c", c=2 * F)
                    nc.scalar.copy(dst[:, :, 0:width], src[:, 4 * h:4 * h + 4, 0:width]).then_inc(staged, 1)

            def tanh_rows(done):
                act.wait_ge(dense_done, done)
                nc.scalar.activation(act_t[:, :], dense[:, :], ACT.Tanh).then_inc(act_ready, 1)

            def keep_x1(row):
                act.wait_ge(turned_done, 2 * row + 2)
                nc.scalar.copy(node_out[:, :].rearrange("p (hf c f) -> p c hf f", hf=2, f=F),
                               turned[:, :].rearrange("p (c hf f) -> p c hf f", hf=2, f=F)).then_inc(x1_ready, 1)
                act.wait_ge(x1_ready, row + 1)
                nc.scalar.copy(cat_of(row, 1), by_tile(node_out)).then_inc(x1_kept, 1)
                for hf in range(2):
                    nc.scalar.copy(feat[0:F, bass.ds(row * BLK + hf * HALF, HALF)],
                                   act_t[hf * F:(hf + 1) * F, :]).then_inc(x1t_kept, 1)

            def keep_turned(count, dst):
                act.wait_ge(turned_done, count)
                tiles = dst.rearrange("p (m two c) -> p two m c", two=2, c=P)
                for half in range(2):
                    src = turned[half * F:(half + 1) * F, :].rearrange("p (m c) -> p m c", c=P)
                    nc.scalar.copy(tiles[:, half], src).then_inc(turned_kept, 1)

            def drain_first(row):
                act.wait_ge(ktile_read, KT * NB * row + KT * NB)
                nc.scalar.copy(agg_t[0:F, :], main[0:F, :]).then_inc(drained1, 1)

            def drain_second(row):
                nc.scalar.copy(rows_of(feat, F, P, row), main[F:P, :]).then_inc(drained1, 1)

            act.wait_ge(cat_cleared, 1)
            act.wait_ge(h_ready, 1)
            stage_block(0, 1, free=False)
            with act.Fori(1, NB - 1) as j:
                act.wait_ge(h_ready, j + 1)
                stage_block(block_at(0, j), j + 1)
            act.wait_ge(h_ready, NB)
            stage_block(block_at(0, NB - 1), 0)
            drain_first(0)
            keep_turned(1, cat_t[0:F, :])
            with act.Fori(1, NB) as row:
                act.wait_ge(turned_done, 2 * row - 1)
                stage_block(block_at(row, 0), wrap(row + 1))
                drain_second(row - 1)
                tanh_rows(row)
                keep_x1(row - 1)
                act.wait_ge(x1_kept, row)
                with act.Fori(1, NB - 1) as j:
                    stage_block(block_at(row, j), wrap(row + 1 + j))
                stage_block(block_at(row, NB - 1), row)
                drain_first(row)
                keep_turned(2 * row + 1, cat_t[0:F, :])
            drain_second(NB - 1)
            tanh_rows(NB)
            keep_x1(NB - 1)

            def bring_features(value, row):
                act.wait_ge(dense_done, value)
                nc.scalar.copy(cat_t[0:F, :], rows_of(feat, 0, F, row)).then_inc(cat_t_in, 1)

            def keep_part(q):
                act.wait_ge(drained2, q - 1)
                act.wait_ge(agg2_in, q)
                nc.scalar.copy(rows_of(feat, F, P, NB - q), agg_t[F:P, :]).then_inc(part_kept, 1)

            def keep_h2(q):
                act.wait_ge(h2_ready, q)
                nc.scalar.copy(cat_of(NB - q, 0), by_tile(node_out)).then_inc(h2_kept, 1)
                act.wait_ge(h2_kept, q)

            act.wait_ge(x1t_kept, 2 * NB)
            act.wait_ge(x1_kept, NB)
            bring_features(NB, NB - 1)
            tanh_rows(NB + 1)
            keep_h2(1)
            stage_block(PASS2, NB - 1)
            keep_turned(2 * NB + 2, rows_of(feat, 0, F, NB - 1))
            bring_features(NB + 1, NB - 2)

            def drain_partial(q, buf):
                act.wait_ge(ktile_read, KT * block_at2(q + 1, 0))
                nc.scalar.copy(agg_t[F:P, :], buf[0:F, :]).then_inc(drained2, 1)

            stage_block(block_at2(2, 0), NB - 1)
            drain_partial(1, main)

            def row2(q, buf, inner):
                tanh_rows(NB + q)
                keep_part(q)
                with inner():
                    with act.Fori(1, q - 1) as j:
                        stage_block(block_at2(q, j), NB - 1 - j)
                keep_h2(q)
                stage_block(block_at2(q, q - 1), wrap(NB - q))
                keep_turned(2 * NB + 2 * q, rows_of(feat, 0, F, NB - q))
                bring_features(NB + q, NB - 1 - q)
                stage_block(block_at2(q + 1, 0), NB - 1)
                act.wait_ge(part_kept, q - 1)
                drain_partial(q, buf)

            with act.Fori(0, NB // 2 - 1) as m:
                row2(2 * m + 2, odd, lambda: act.If(m > 0))
                row2(2 * m + 3, main, nullcontext)

            def drain_even(t, buf):
                act.wait_ge(ktile_read, KT * block_at3(t + 1, 0))
                nc.scalar.copy(agg_t[0:F, :], buf[0:F, :]).then_inc(drained3, 1)

            tanh_rows(2 * NB)
            keep_part(NB)
            with act.Fori(1, NB - 1) as j:
                stage_block(block_at3(0, j), NB - 1 - j, width=F)
            keep_h2(NB)
            stage_block(block_at3(0, NB - 1), 0, width=F)
            keep_turned(4 * NB, rows_of(feat, 0, F, 0))
            bring_features(2 * NB, NB - 1)
            drain_even(0, own)
            act.wait_ge(turned_kept, 4 * NB)
            with act.Fori(1, NB) as t:
                with act.Fori(0, NB - t) as j:
                    stage_block(block_at3(t, j), wrap(NB - 1 - t - j), width=F)
                bring_features(2 * NB + t, NB - 1 - t)
                drain_even(t, main)

        @block.vector
        def _(dve):
            def norm_first(i, src):
                def after(k):
                    dve.wait_ge(norm_step, 6 * i + k)

                nc.vector.tensor_reduce(total[:, :], src, AX.X, ALU.add).then_inc(norm_step, 1)
                after(1)
                nc.vector.tensor_scalar(negmean[:, :], total[:, :], -1.0 / F, None, ALU.mult).then_inc(norm_step, 1)
                after(2)
                nc.vector.tensor_tensor(by_tile(centred), src, spread(negmean[:, :]), ALU.add).then_inc(norm_step, 1)
                after(3)
                nc.vector.tensor_tensor(by_tile(square), by_tile(centred), by_tile(centred), ALU.mult).then_inc(norm_step, 1)
                after(4)
                nc.vector.tensor_reduce(sqsum[:, :], by_tile(square), AX.X, ALU.add).then_inc(norm_step, 1)
                after(5)
                nc.vector.tensor_scalar(var[:, :], sqsum[:, :], 1.0 / F, EPS, ALU.mult, ALU.add).then_inc(norm_step, 1)

            def norm_last(i, dst):
                dve.wait_ge(rstd_ready, i + 1)
                return nc.vector.scalar_tensor_tensor(out=dst, in0=by_tile(centred), scalar=0.0,
                                                      in1=spread(rstd[:, :]), op0=ALU.max, op1=ALU.mult)

            def count(done, dst, tiles):
                dve.wait_ge(counted, done)
                nc.vector.scalar_tensor_tensor(out=dst[:, :], in0=tiles.rearrange("p s r -> p (s r)"), scalar=0.0,
                                               in1=tally[:, :], op0=ALU.not_equal, op1=ALU.add).then_inc(counted, 1)

            def count_ring(row, j):
                for c in range(KT // 2):
                    for s in (2 * c, 2 * c + 1):
                        dve.wait_ge(ring_full[s], 16 * ((NB - 1) * row + j) + 16)
                    count(COUNTS * row + 1 + 4 * j + c, tally, ring[:, 2 * c:2 * c + 2, :])

            def count_diag(row):
                for c in range(KT // 2):
                    dve.wait_ge(diag_full[c], 16 * row + 16)
                    dst = tally if c < KT // 2 - 1 else tally_out
                    count(COUNTS * row + 1 + 4 * (NB - 1) + c, dst, diag[:, 2 * c:2 * c + 2, :])

            def take_counts(row):
                dve.wait_ge(counts_done, row + 1)
                nc.vector.tensor_copy(degree[:, bass.ds(row * KT, KT)], dense[:, 0:KT]).then_inc(count_read, 1)

            def add_own(row):
                dve.wait_ge(own_done, row + 1)
                dve.wait_ge(drained1, 2 * row + 2)
                part = rows_of(feat, F, P, row)
                nc.vector.tensor_tensor(part, part, own[F:P, :], ALU.add).then_inc(own_added, 1)
                dve.wait_ge(own_added, 2 * row + 3)
                nc.vector.tensor_tensor(part, part, own[0:F, :], ALU.add).then_inc(own_added, 1)

            def drain_odd(row):
                dve.wait_ge(ktile_read, KT * NB * row + KT * NB)
                nc.vector.tensor_copy(cat_t[F:P, :], odd[F:P, :]).then_inc(odd_drained, 1)

            dve.sem_inc(count_read, 1)
            dve.sem_inc(own_added, 2)
            dve.sem_inc(out_step, 4)

            def x_first(i, g):
                dve.wait_ge(x_in[g], 16)
                norm_first(i, nodes_of(xres, g))

            nc.vector.memset(cat[:, :].rearrange("p (k c) -> p k c", c=2 * F)[:, :, F:2 * F], 0.0).then_inc(cat_cleared, 1)
            x_first(0, 1)
            nc.vector.memset(tally[:, :], 0.0).then_inc(counted, 1)
            norm_last(0, cat_of(1, 0)).then_inc(h_ready, 1)
            for j in range(NB - 1):
                x_first(j + 1, (j + 2) % NB)
                count_ring(0, j)
                norm_last(j + 1, cat_of((j + 2) % NB, 0)).then_inc(h_ready, 1)
            count_diag(0)
            drain_odd(0)
            with dve.Fori(1, NB) as row:
                dve.wait_ge(counted, COUNTS * row)
                nc.vector.memset(tally[:, :], 0.0).then_inc(counted, 1)
                with dve.Fori(0, NB - 1) as j:
                    count_ring(row, j)
                dve.wait_ge(counts_done, row)
                count_diag(row)
                take_counts(row - 1)
                add_own(row - 1)
                drain_odd(row)
            take_counts(NB - 1)
            add_own(NB - 1)

            def y_and_norm(q, row):
                y = nodes_of(xres, row)
                y = y.rearrange("p (hf c) f -> p hf c f", hf=2)
                x2 = turned[:, :].rearrange("p (c hf f) -> p hf c f", hf=2, f=F)
                dve.wait_ge(turned_done, 2 * NB + 2 * q - 1)
                nc.vector.tensor_tensor(y, y, x2, ALU.add).then_inc(y_ready, 1)
                dve.wait_ge(y_ready, q)
                norm_first(NB + q - 1, nodes_of(xres, wrap(row)))

            def h2_rows(q):
                norm_last(NB + q - 1, by_tile(node_out)).then_inc(h2_ready, 1)

            dve.wait_ge(own_added, 2 * NB + 2)
            dve.wait_ge(dense_done, NB)
            nc.vector.tensor_copy(cat_t[F:P, :], rows_of(feat, F, P, NB - 1)).then_inc(agg2_in, 1)
            dve.wait_ge(agg2_in, 1)
            nc.vector.memset(rows_of(feat, F, P, NB - 1), 0.0).then_inc(part_cleared, 1)
            y_and_norm(1, NB - 1)
            dve.wait_ge(x1_kept, NB)
            dve.wait_ge(own_done, NB)
            h2_rows(1)
            dve.wait_ge(count_read, NB + 1)
            nc.vector.tensor_scalar(degree[:, :], degree[:, :], 1.0, None, ALU.max).then_inc(degree_ready, 1)

            def row2(q, before):
                row = settled(dve, NB - q)
                dve.wait_ge(ktile_read, KT * block_at2(q, 0))
                dve.wait_ge(dense_done, NB + q - 1)
                nc.vector.tensor_tensor(cat_t[F:P, :], rows_of(feat, F, P, row), before[F:P, :],
                                        ALU.add).then_inc(agg2_in, 1)
                y_and_norm(q, row)
                dve.wait_ge(h2_kept, q - 1)
                dve.wait_ge(turned_done, 2 * NB + 2 * (q - 1))
                h2_rows(q)

            with dve.Fori(0, NB // 2 - 1) as m:
                row2(2 * m + 2, main)
                row2(2 * m + 3, odd)
            row2(NB, main)
            dve.wait_ge(invroot_ready, 1)
            nc.vector.tensor_scalar(degree[:, :], degree[:, :], -1.0, None, ALU.mult).then_inc(degree_ready, 1)
            dve.wait_ge(part_cleared, 1)
            dve.wait_ge(degree_ready, 2)

            def row3(t, buf):
                row = settled(dve, NB - 1 - t)
                dve.wait_ge(ktile_read, KT * block_at3(t + 1, 0))
                dve.wait_ge(part_kept, NB - 1)
                dve.wait_ge(dense_done, 2 * NB + t)
                nc.vector.tensor_tensor(agg_t[F:P, :], rows_of(feat, F, P, row), buf[F:P, :],
                                        ALU.add).then_inc(agg3_in, 1)
                dve.wait_ge(dense_done, 2 * NB + 1 + t)
                scale = degree[:, bass.ds(row * KT, KT)].unsqueeze(2).to_broadcast([P, KT, F])
                nc.vector.tensor_tensor(by_tile(square), by_tile(turned), scale, ALU.mult).then_inc(out_step, 1)
                dve.wait_ge(out_step, 4 * t + 5)
                nc.vector.tensor_tensor(centred[:, :], square[:, :], dense[:, :], ALU.add).then_inc(out_step, 1)
                dve.wait_ge(out_step, 4 * t + 6)
                nc.vector.tensor_tensor(by_tile(square), by_tile(centred),
                                        bias[:, :].unsqueeze(1).to_broadcast([P, KT, F]), ALU.add).then_inc(out_step, 1)
                dve.wait_ge(out_step, 4 * t + 7)
                y = nodes_of(xres, row)
                nc.vector.scalar_tensor_tensor(out=y, in0=by_tile(square), scalar=0.0, in1=y,
                                               op0=ALU.max, op1=ALU.add).then_inc(out_step, 1)

            row3(0, own)
            with dve.Fori(1, NB) as t:
                row3(t, odd)

        @block.gpsimd
        def _(pool):
            nc.gpsimd.memset(ident[:, :], 0.0).then_inc(const_made, 1)
            nc.gpsimd.memset(zeros[:, :], 0.0).then_inc(const_made, 1)
            nc.gpsimd.memset(ones[:, :], 1.0).then_inc(const_made, 1)
            pool.wait_ge(const_made, 3)
            nc.gpsimd.affine_select(out=ident[:, :], in_=ident[:, :], compare_op=ALU.not_equal, fill=1.0, base=0,
                                    pattern=[[-1, P]], channel_multiplier=1).then_inc(const_made, 1)
            nc.gpsimd.memset(minus_half[:, :], -0.5).then_inc(const_made, 1)
            pool.wait_ge(const_made, 5)

            def power(i):
                pool.wait_ge(norm_step, 6 * i + 6)
                nc.gpsimd.tensor_tensor(rstd[:, :], var[:, :], minus_half[:, 0:KT], ALU.pow).then_inc(rstd_ready, 1)

            with pool.Fori(0, NB + 1) as i:
                power(i)
            pool.wait_ge(degree_ready, 1)
            nc.gpsimd.tensor_tensor(degree[:, :], degree[:, :], minus_half[:, :], ALU.pow).then_inc(invroot_ready, 1)
            with pool.Fori(NB + 1, 2 * NB) as i:
                power(i)
            with pool.Fori(0, NB) as t:
                first = settled(pool, (NB - 1 - t) * GW)
                pool.wait_ge(out_step, 4 * t + 8)
                rows = bass.ds(first, GW)
                pool.dma_start(out_d[:, rows], xres[:, rows]).then_inc(out_stored, 16)
            pool.wait_ge(out_stored, 16 * NB)


def kernel(**inputs):
    import numpy as np
    import concourse.bacc as bacc
    from concourse.bass_utils import run_bass_kernel_spmd

    n, f = inputs["x"].shape
    nb = n // BLK

    def node_major(a):
        return np.ascontiguousarray(a.reshape(n // P, P, f).transpose(1, 0, 2).reshape(P, -1))

    adj = np.asarray(inputs["adj"]).reshape(nb, BLK, nb, KT, P)
    arrays = {
        "x": node_major(np.asarray(inputs["x"])),
        "adj": np.ascontiguousarray(adj.transpose(0, 2, 3, 4, 1)).reshape(nb * nb * KT, P, BLK),
        "w0": np.ascontiguousarray(inputs["L0_gnn_W"][0]),
        "w1": np.ascontiguousarray(inputs["L0_gnn_W"][1]),
        "w3": np.ascontiguousarray(inputs["L1_gnn_W"]),
        "b": np.ascontiguousarray(inputs["L1_gnn_b"]),
    }
    nc = bacc.Bacc("TRN2", target_bir_lowering=False, num_devices=1)
    args = [nc.dram_tensor("in_" + name, a.shape, mybir.dt.from_np(a.dtype), kind="ExternalInput").ap()
            for name, a in arrays.items()]
    out = nc.dram_tensor("out", (P, n // P * f), F32, kind="ExternalOutput").ap()
    gnn_program(nc, *args, out)
    r = run_bass_kernel_spmd(nc, [{"in_" + name: a for name, a in arrays.items()}], core_ids=[0])
    return r.results[0]["out"].reshape(P, n // P, f).transpose(1, 0, 2).reshape(n, f)
```
